# Optimizing a Trainium2 kernel written in Bass

```python
import numpy as np
import jax
import jax.numpy as jnp

def _softmax(x, axis=-1):
    return jax.nn.softmax(x, axis=axis)

def _gelu(x):
    return jax.nn.gelu(x, approximate=True)

def _silu(x):
    return jax.nn.silu(x)

def _sigmoid(x):
    return jax.nn.sigmoid(x)

def _layernorm(x, axis=-1, eps=1e-05):
    m = jnp.mean(x, axis=axis, keepdims=True)
    v = jnp.var(x, axis=axis, keepdims=True)
    return (x - m) / jnp.sqrt(v + eps)

def _scatter_add(tgt, idx, src, axis=0):
    return tgt.at[idx].add(src)

def _segment_sum(src, seg, n):
    return jax.ops.segment_sum(src, seg, n)
kernel_name = 'mk_adaln_d1_jaxref_r8_0b6c38'

def setup_inputs(seed: int=0):
    np.random.seed(seed)
    _w = jnp.asarray

    def _L0_attn_setup():
        import jax, jax.numpy as jnp
        import numpy as np
        import math
        D_MODEL = 256
        N_HEADS = 16
        D_HEAD = 128
        BATCH = 2
        SEQ = 256
        key = jax.random.key(seed)
        ks = jax.random.split(key, 5)
        std = 0.02
        x = jax.random.normal(ks[0], (BATCH, SEQ, D_MODEL), dtype=jnp.float32)
        W_Q = std * jax.random.normal(ks[1], (N_HEADS, D_HEAD, D_MODEL), dtype=jnp.float32)
        W_K = std * jax.random.normal(ks[2], (N_HEADS, D_HEAD, D_MODEL), dtype=jnp.float32)
        W_V = std * jax.random.normal(ks[3], (N_HEADS, D_HEAD, D_MODEL), dtype=jnp.float32)
        W_O = std * jax.random.normal(ks[4], (N_HEADS, D_MODEL, D_HEAD), dtype=jnp.float32)
        return {'x': x, 'W_Q': W_Q, 'W_K': W_K, 'W_V': W_V, 'W_O': W_O}
    _L0_attn_in = _L0_attn_setup()

    def _L0_ffn_setup():
        import jax, jax.numpy as jnp
        import numpy as np
        B, S, D = (4, 256, 256)
        E = 8
        N_SHARE = 2
        N_ROUTED = E - N_SHARE
        H = 1024 // E
        key = jax.random.key(seed)
        ks = jax.random.split(key, 12)
        s = 0.02
        return {'x': jax.random.normal(ks[0], (B, S, D), jnp.float32), 'Wg': jax.random.normal(ks[1], (D, E), jnp.float32) * s, 'bg': jnp.zeros((E,), jnp.float32), 'Wgate': jax.random.normal(ks[2], (N_ROUTED, D, H), jnp.float32) * s, 'bgate': jnp.zeros((N_ROUTED, H), jnp.float32), 'Wup': jax.random.normal(ks[3], (N_ROUTED, D, H), jnp.float32) * s, 'bup': jnp.zeros((N_ROUTED, H), jnp.float32), 'Wdown': jax.random.normal(ks[4], (N_ROUTED, H, D), jnp.float32) * s, 'bdown': jnp.zeros((N_ROUTED, D), jnp.float32), 'Ws_up': jax.random.normal(ks[5], (D, N_SHARE * H), jnp.float32) * s, 'bs_up': jnp.zeros((N_SHARE * H,), jnp.float32), 'Ws_down': jax.random.normal(ks[6], (N_SHARE * H, D), jnp.float32) * s, 'bs_down': jnp.zeros((D,), jnp.float32)}
    _L0_ffn_in = _L0_ffn_setup()
    _L0_c = _w((lambda *s: np.random.randn(*s).astype(np.float32) * 0.05)(8, 256))
    _L0_wmod = _w((lambda *s: np.random.randn(*s).astype(np.float32) * 0.05)(256, 6 * 256) * 256 ** (-0.5))
    _d = {'L0_attn_x': _L0_attn_in['x'], 'L0_attn_W_Q': _L0_attn_in['W_Q'], 'L0_attn_W_K': _L0_attn_in['W_K'], 'L0_attn_W_V': _L0_attn_in['W_V'], 'L0_attn_W_O': _L0_attn_in['W_O'], 'L0_ffn_Wg': _L0_ffn_in['Wg'], 'L0_ffn_bg': _L0_ffn_in['bg'], 'L0_ffn_Wgate': _L0_ffn_in['Wgate'], 'L0_ffn_bgate': _L0_ffn_in['bgate'], 'L0_ffn_Wup': _L0_ffn_in['Wup'], 'L0_ffn_bup': _L0_ffn_in['bup'], 'L0_ffn_Wdown': _L0_ffn_in['Wdown'], 'L0_ffn_bdown': _L0_ffn_in['bdown'], 'L0_ffn_Ws_up': _L0_ffn_in['Ws_up'], 'L0_ffn_bs_up': _L0_ffn_in['bs_up'], 'L0_ffn_Ws_down': _L0_ffn_in['Ws_down'], 'L0_ffn_bs_down': _L0_ffn_in['bs_down'], 'L0_c': _L0_c, 'L0_wmod': _L0_wmod}
    _x0 = _d['L0_attn_x']
    _d['L0_attn_x'] = jax.random.normal(jax.random.fold_in(jax.random.key(seed), 1), (8, 512, 256), dtype=_x0.dtype)
    del _x0
    return _d

def reference(L0_attn_x, L0_attn_W_Q, L0_attn_W_K, L0_attn_W_V, L0_attn_W_O, L0_ffn_Wg, L0_ffn_bg, L0_ffn_Wgate, L0_ffn_bgate, L0_ffn_Wup, L0_ffn_bup, L0_ffn_Wdown, L0_ffn_bdown, L0_ffn_Ws_up, L0_ffn_bs_up, L0_ffn_Ws_down, L0_ffn_bs_down, L0_c, L0_wmod):

    def _L0_attn_ref(x, W_Q, W_K, W_V, W_O):
        import jax, jax.numpy as jnp
        import numpy as np
        import math
        D_MODEL = 256
        N_HEADS = 16
        D_HEAD = 128
        BATCH = 2
        SEQ = 256
        d_head = W_Q.shape[1]
        seq_len = x.shape[1]
        scale = 1.0 / math.sqrt(d_head)
        q = jnp.einsum('bsd,hed->bhse', x, W_Q)
        k = jnp.einsum('bsd,hed->bhse', x, W_K)
        v = jnp.einsum('bsd,hed->bhse', x, W_V)
        scores = jnp.einsum('bhse,bhme->bhsm', q, k) * scale
        causal = jnp.triu(jnp.ones((seq_len, seq_len), dtype=bool), k=1)
        scores = jnp.where(causal, jnp.float32(-1000000000.0), scores)
        pattern = jax.nn.softmax(scores, axis=-1)
        z = jnp.einsum('bhsm,bhme->bhse', pattern, v)
        out = jnp.einsum('bhse,hde->bsd', z, W_O)
        return out

    def _L0_ffn_ref(x, Wg, bg, Wgate, bgate, Wup, bup, Wdown, bdown, Ws_up, bs_up, Ws_down, bs_down):
        import jax, jax.numpy as jnp
        import numpy as np
        B, S, D = (4, 256, 256)
        E = 8
        N_SHARE = 2
        N_ROUTED = E - N_SHARE
        H = 1024 // E
        b, s, d = x.shape
        T = b * s
        n = Wgate.shape[0]
        xf = x.reshape(T, d)
        gate = xf @ Wg + bg
        vals, ids = jax.lax.top_k(gate, n)
        rows = jnp.arange(T)[:, None]
        masked = jnp.full_like(gate, -jnp.inf).at[rows, ids].set(vals)
        probs = jax.nn.softmax(masked, axis=-1)
        routed_mask = (ids[:, :, None] == jnp.arange(n)).any(axis=1)
        w = probs[:, :n] * routed_mask
        g = jnp.einsum('td,ndh->tnh', xf, Wgate) + bgate
        u = jnp.einsum('td,ndh->tnh', xf, Wup) + bup
        h = jax.nn.silu(g) * u
        eo = jnp.einsum('tnh,nhd->tnd', h, Wdown) + bdown
        routed_out = jnp.einsum('tnd,tn->td', eo, w)
        share = jax.nn.silu(xf @ Ws_up + bs_up) @ Ws_down + bs_down
        return (routed_out + share).reshape(b, s, d)
    x = L0_attn_x
    mod = (_silu(L0_c) @ L0_wmod).reshape(L0_c.shape[0], 6, 1, -1)
    sa, ca, ga, sb, cb, gb = (mod[:, 0], mod[:, 1], mod[:, 2], mod[:, 3], mod[:, 4], mod[:, 5])
    ga = (2 * (ga >= 0) - 1) * jnp.maximum(jnp.abs(ga), 0.25)
    gb = (2 * (gb >= 0) - 1) * jnp.maximum(jnp.abs(gb), 0.25)
    h = _layernorm(x, axis=-1) * (1 + ca) + sa
    x = x + ga * _L0_attn_ref(h, L0_attn_W_Q, L0_attn_W_K, L0_attn_W_V, L0_attn_W_O)
    h = _layernorm(x, axis=-1) * (1 + cb) + sb
    x = x + gb * _L0_ffn_ref(h, L0_ffn_Wg, L0_ffn_bg, L0_ffn_Wgate, L0_ffn_bgate, L0_ffn_Wup, L0_ffn_bup, L0_ffn_Wdown, L0_ffn_bdown, L0_ffn_Ws_up, L0_ffn_bs_up, L0_ffn_Ws_down, L0_ffn_bs_down)
    return x

_drawn_inputs = setup_inputs


def setup_inputs(seed=0):
    import zlib

    import numpy as np

    out = dict(_drawn_inputs(seed))
    spreads = {'L0_ffn_bg': (0.0, 0.8),
     'L0_ffn_bgate': (0.0, 0.8),
     'L0_ffn_bup': (0.0, 0.8),
     'L0_ffn_bdown': (0.0, 0.8),
     'L0_ffn_bs_up': (0.0, 0.8),
     'L0_ffn_bs_down': (0.0, 1.076)}
    factors = {'L0_attn_W_Q': 8.0,
     'L0_attn_W_K': 8.0,
     'L0_attn_W_V': 6.8,
     'L0_attn_W_O': 6.717,
     'L0_ffn_Wg': 8.0,
     'L0_ffn_Wgate': 8.0,
     'L0_ffn_Wup': 8.0,
     'L0_ffn_Wdown': 8.0,
     'L0_ffn_Ws_up': 4.298,
     'L0_ffn_Ws_down': 4.051}
    for name, (base, spread) in spreads.items():
        noise = np.random.default_rng([zlib.crc32(name.encode()), seed]).standard_normal(out[name].shape)
        drawn = base * np.exp(spread * noise) if base else spread * noise
        out[name] = jnp.asarray(drawn.astype(out[name].dtype))
    for name, factor in factors.items():
        out[name] = (out[name] * factor).astype(out[name].dtype)
    return out
```

```python
from contextlib import ExitStack

import concourse.bass as bass
from concourse import mybir

ALU = mybir.AluOpType
ACT = mybir.ActivationFunctionType
AX_X = mybir.AxisListType.X
F32 = mybir.dt.float32
F32R = mybir.dt.float32r

P = 128
DMA_INC = 16
LN_EPS = 1e-5
GATE_MIN = 0.25
MASKED = 1e30
HUGE = 3e38
PASSES = ((0, 0), (0, 1), (1, 0))

S_BANK = ({1: 0, 0: 2, 2: 2, 3: 1}, {1: 4, 0: 5, 2: 5, 3: 3})
S_COL = {1: 0, 0: 0, 2: P, 3: 0}
S_ORDER = (1, 0, 2, 3)
Z_BANK = (3, 1)
QK_BANK = ((4, 5), (0, 2))
V_BANK = (0, 3)
T_BANK = ((1, 2, 0), (3, 4, 5))
ACC_BANK = 6
T_HOLDS = (((0, 0),), ((1, 0), (3, 3 * P)), ((2, 0),))
T_WIDTH = (4 * P, 4 * P, 2 * P)
PT_AT = {0: 0, 1: 4 * P, 3: 7 * P, 2: 8 * P}


def tile_at(i):
    return P * (i * (i + 1) // 2)


def alone(eng, semaphore, value):
    eng.wait_ge(semaphore, value)
    eng.nop(nofuse=True)


def rows(dram, b):
    return dram[b].rearrange("(t p) d -> p t d", p=P)


def attention_layer(nc, psum, stage, mod_t, gates, ident, x, wqk_d, wv_d, wo_d, c_d, wmod_d, up_d, up_loaded, x1):
    B, SEQ, D = x.shape
    H = wo_d.shape[1] // D
    NT = SEQ // P
    DC = D // P
    PAIRS = H // 2
    SW = tile_at(NT)
    HEADS = B * H
    SCALE = 1.0 / float(P) ** 0.5

    with ExitStack() as ctx:
        def sb(name, shape, dt=F32):
            return ctx.enter_context(nc.sbuf_tensor(name, shape, dt))

        def sem(name):
            return ctx.enter_context(nc.semaphore(name))

        def pair_of(name, shape):
            return [sb(name + "_hi", shape, F32R), sb(name + "_lo", shape, F32R)]

        wqk = sb("wqk", [P, H + 1, 2 * DC * P])
        wv = pair_of("wv", [P, PAIRS, DC, 2 * P])
        wo = pair_of("wo", [P, H, D])
        ws = pair_of("ws", [P, 2, DC, P])
        xin = sb("xin", [P, NT, D])
        ht32 = sb("ht32", [P, DC, SEQ])
        ht = pair_of("ht", [P, DC, SEQ])
        stats = sb("stats", [P, NT, 6])
        mv = sb("mv", [P, NT, 2])
        rstd = sb("rstd", [P, NT])
        minus_half = sb("minus_half", [P, NT])
        qt = pair_of("qt", [P, SEQ])
        kt = pair_of("kt", [P, SEQ])
        v = pair_of("v", [P, NT, 2 * P])
        probs = sb("probs", [P, 2, SW])
        pt = pair_of("pt", [P, SW])
        z = pair_of("z", [P, SEQ])
        neg_max = sb("neg_max", [P, 2, NT])
        row_sum = sb("row_sum", [P, 2, NT])
        inv_sum = sb("inv_sum", [P, 2, NT])
        xres = sb("xres", [P, NT, D])
        y = sb("y", [P, NT, D])
        act_c = sb("act_c", [P, DC, B])
        gates8 = sb("gates8", [B, 2 * D])
        gates8s = sb("gates8s", [B, 2 * D])
        gates8a = sb("gates8a", [B, 2 * D])
        mask = sb("mask", [P, SEQ])
        wmod = stage[:, 0:DC * 6 * D].rearrange("p (c n) -> p c n", c=DC)
        pick = probs[0:B, 0, 0:B * P].rearrange("p (b m) -> p b m", b=B)

        c_loaded = sem("c_loaded")
        wmod_loaded = sem("wmod_loaded")
        wqk_loaded = sem("wqk_loaded")
        wv_loaded = sem("wv_loaded")
        wo_loaded = sem("wo_loaded")
        x_loaded = sem("x_loaded")
        xres_loaded = sem("xres_loaded")
        consts = sem("consts")
        c_act = sem("c_act")
        mod_psum = sem("mod_psum")
        mod_ready = sem("mod_ready")
        g8 = sem("g8")
        g8_ready = sem("g8_ready")
        gate_psum = sem("gate_psum")
        gate_copied = sem("gate_copied")
        wq_scaled = sem("wq_scaled")
        wv_hi = sem("wv_hi")
        wv_split = sem("wv_split")
        wo_hi = sem("wo_hi")
        wo_split = sem("wo_split")
        ln_chain = sem("ln_chain")
        ln_var = sem("ln_var")
        ln_rstd = sem("ln_rstd")
        ln_ready = sem("ln_ready")
        ln_psum = sem("ln_psum")
        ht32_ready = sem("ht32_ready")
        ht_hi = sem("ht_hi")
        ht_split = sem("ht_split")
        w_hi = sem("w_hi")
        w_staged = sem("w_staged")
        qk_psum = sem("qk_psum")
        qk_hi = sem("qk_hi")
        qk_split = sem("qk_split")
        v_psum = sem("v_psum")
        v_hi = sem("v_hi")
        v_split = sem("v_split")
        s_psum = sem("s_psum")
        s_masked = sem("s_masked")
        p_exp = sem("p_exp")
        sum_inv = sem("sum_inv")
        p_norm = sem("p_norm")
        t_psum = sem("t_psum")
        t_hi = sem("t_hi")
        t_split = sem("t_split")
        z_psum = sem("z_psum")
        z_hi = sem("z_hi")
        z_split = sem("z_split")
        o_done = sem("o_done")
        acc_zero = sem("acc_zero")
        acc_gated = sem("acc_gated")
        y_free = sem("y_free")
        x1_ready = sem("x1_ready")

        acc = psum[:, ACC_BANK:ACC_BANK + 2, :].rearrange("p k (t n) -> p (k t) n", t=2)

        def walk(eng, step, batch_begin, last_begin, tail):
            step(0, 0, 0, 0, first=True)
            with eng.Fori(0, B - 1) as b:
                batch_begin(b)
                with eng.Fori(0, PAIRS - 1) as p:
                    step(b * H + p * 2 + 1, p * 2 + 1, 1, b)
                    step(b * H + p * 2 + 2, p * 2 + 2, 0, b, pair=p + 1)
                step(b * H + H - 1, H - 1, 1, b, turn=True)
                step(b * H + H, 0, 0, b + 1, new=True)
            last_begin()
            with eng.Fori(0, PAIRS - 1) as p:
                step(p * 2 + (B - 1) * H + 1, p * 2 + 1, 1, B - 1)
                step(p * 2 + (B - 1) * H + 2, p * 2 + 2, 0, B - 1, pair=p + 1)
            step(HEADS - 1, H - 1, 1, B - 1, last=True)
            tail()

        block = ctx.enter_context(nc.Block())

        @block.sync
        def _(sp):
            sp.dma_start(act_c[:], c_d).then_inc(c_loaded, DMA_INC)
            sp.dma_start(stage[:, 0:DC * 6 * D], wmod_d).then_inc(wmod_loaded, DMA_INC)
            sp.dma_start(xin[:], rows(x, 0)).then_inc(x_loaded, DMA_INC)
            sp.dma_start(wqk[:, 0:H, :], wqk_d).then_inc(wqk_loaded, DMA_INC)
            sp.wait_ge(mod_psum, 2)
            sp.dma_start(stage[:], wv_d).then_inc(wv_loaded, DMA_INC)
            sp.wait_ge(wv_split, 1)
            sp.dma_start(stage[:], wo_d).then_inc(wo_loaded, DMA_INC)
            sp.wait_ge(wo_split, 1)
            sp.dma_start(stage[:, 0:up_d.shape[1]], up_d).then_inc(up_loaded, DMA_INC)
            with sp.Fori(0, B - 1) as b:
                sp.wait_ge(ln_psum, b * 2 + 2)
                sp.dma_start(xin[:], rows(x, b + 1)).then_inc(x_loaded, DMA_INC)
                sp.dma_start(xres[:], rows(x, b)).then_inc(xres_loaded, DMA_INC)
                sp.wait_ge(x1_ready, b + 1)
                sp.dma_start(rows(x1, b), y[:]).then_inc(y_free, DMA_INC)
            sp.dma_start(xres[:], rows(x, B - 1)).then_inc(xres_loaded, DMA_INC)
            sp.wait_ge(x1_ready, B)
            sp.dma_start(rows(x1, B - 1), y[:]).then_inc(y_free, DMA_INC)
            sp.wait_ge(y_free, DMA_INC * B + DMA_INC)

        @block.gpsimd
        def _(pool):
            pool.memset(ident[:], 0.0).then_inc(consts, 1)
            pool.memset(mask[:], 0.0).then_inc(consts, 1)
            pool.memset(pick, 0.0).then_inc(consts, 1)
            pool.wait_ge(consts, 3)
            pool.affine_select(out=ident[:], in_=ident[:], compare_op=ALU.not_equal, fill=1.0, base=0,
                               pattern=[[-1, P]], channel_multiplier=1).then_inc(consts, 1)
            pool.affine_select(out=mask[:, SEQ - P:], in_=mask[:, SEQ - P:], compare_op=ALU.is_ge, fill=MASKED,
                               base=0, pattern=[[-1, P]], channel_multiplier=1).then_inc(consts, 1)
            pool.affine_select(out=pick, in_=pick, compare_op=ALU.not_equal, fill=1.0, base=0,
                               pattern=[[-1, B], [0, P]], channel_multiplier=1).then_inc(consts, 1)
            pool.memset(minus_half[:], -0.5).then_inc(consts, 1)
            pool.wait_ge(consts, 7)

            def layer_norm_rstd(b):
                pool.wait_ge(ln_var, b + 1)
                pool.tensor_tensor(rstd[:], mv[:, :, 1], minus_half[:], ALU.pow).then_inc(ln_rstd, 1)

            def stage_weights(i, h):
                if not (isinstance(i, int) and i == 0):
                    alone(pool, qk_psum, i * 2)
                src = wqk[:, h, :].rearrange("p (a c e) -> p a c e", a=2, c=DC)
                pool.tensor_copy(ws[0][:], src).then_inc(w_hi, 1)
                alone(pool, w_hi, i + 1)
                pool.tensor_tensor(ws[1][:], src, ws[0][:], ALU.subtract).then_inc(w_staged, 1)

            layer_norm_rstd(0)
            pool.wait_ge(wq_scaled, 1)
            pool.tensor_copy(wqk[:, H, :], wqk[:, 0, :]).then_inc(consts, 1)
            pool.wait_ge(consts, 8)
            stage_weights(0, 0)
            stage_weights(1, 1)

            def step(i, h, odd, b, pair=0, first=False, turn=False, new=False, last=False):
                alone(pool, sum_inv, i + 1)
                for t in S_ORDER:
                    row = probs[:, odd, tile_at(t):tile_at(t + 1)]
                    pool.tensor_scalar(row, row, inv_sum[:, odd, t:t + 1], 1.0, ALU.mult, ALU.mult).then_inc(p_norm, 1)
                if new:
                    add_residual(b - 1)
                if not last:
                    stage_weights(i + 2, 1 if turn else h + 2)

            def add_residual(b):
                pool.wait_ge(acc_gated, b + 2)
                pool.wait_ge(xres_loaded, b * DMA_INC + DMA_INC)
                pool.tensor_tensor(y[:], y[:], xres[:], ALU.add).then_inc(x1_ready, 1)

            walk(pool, step, lambda b: layer_norm_rstd(b + 1), lambda: None, lambda: add_residual(B - 1))

        @block.scalar
        def _(act):
            act.wait_ge(c_loaded, DMA_INC)
            act.activation(act_c[:], act_c[:], ACT.Silu).then_inc(c_act, 1)

            def ht_evacuate(b):
                for c in range(DC):
                    act.wait_ge(ln_psum, b * DC + c + 1)
                    act.activation(ht32[:, c, :], psum[:, ACC_BANK + c, :], ACT.Identity,
                                   bias=mod_t[:, c, bass.ds(b, 1)],
                                   scale=mod_t[:, DC + c, bass.ds(b, 1)]).then_inc(ht32_ready, 1)

            def ht_split_hi(b):
                act.wait_ge(ht32_ready, b * DC + DC)
                act.activation(ht[0][:], ht32[:], ACT.Copy).then_inc(ht_hi, 1)

            def qk_evacuate(i, odd):
                for n, dst in enumerate((qt, kt)):
                    act.wait_ge(qk_psum, i * 2 + n + 1)
                    act.activation(dst[0][:], psum[:, QK_BANK[1 - odd][n], :], ACT.Copy).then_inc(qk_hi, 1)

            act.wait_ge(mod_ready, 1)
            ht_evacuate(0)
            ht_split_hi(0)
            qk_evacuate(0, 0)
            for b in range(B):
                act.wait_ge(gate_psum, b + 1)
                act.activation(gates[:, b, :], psum[:, 3 + b % 3, :], ACT.Copy).then_inc(gate_copied, 1)
            act.wait_ge(wv_loaded, DMA_INC)
            act.activation(wv[0][:].rearrange("p a c n -> p (a c n)"), stage[:], ACT.Copy).then_inc(wv_hi, 1)

            def step(i, h, odd, b, pair=0, first=False, turn=False, new=False, last=False):
                if turn:
                    act.wait_ge(v_psum, b * H + H)
                    act.wait_ge(qk_psum, b * 2 * H + 2 * H)
                    ht_split_hi(b + 1)
                for n, t in enumerate(S_ORDER):
                    act.wait_ge(s_masked, i * NT + n + 1)
                    row = probs[:, odd, tile_at(t):tile_at(t + 1)]
                    act.activation(row, row, ACT.Exp, bias=neg_max[:, odd, t:t + 1], scale=-1.0,
                                   accum_out=row_sum[:, odd, t:t + 1]).then_inc(p_exp, 1)
                if not first:
                    z_evacuate(i - 1, 1 - odd)
                if not last:
                    qk_evacuate(i + 1, 1 - odd)
                if not odd:
                    for half in range(2):
                        act.wait_ge(v_psum, i + half + 1)
                        act.activation(v[0][:, 2 * half:2 * half + 2, :].rearrange("p t n -> p (t n)"),
                                       psum[:, V_BANK[half], :], ACT.Copy).then_inc(v_hi, 1)
                for n in range(3):
                    act.wait_ge(t_psum, i * 3 + n + 1)
                    act.activation(pt[0][:, n * 4 * P:n * 4 * P + T_WIDTH[n]],
                                   psum[:, T_BANK[odd][n], 0:T_WIDTH[n]], ACT.Copy).then_inc(t_hi, 1)
                if first:
                    act.wait_ge(wo_loaded, DMA_INC)
                    act.activation(wo[0][:].rearrange("p a n -> p (a n)"), stage[:], ACT.Copy).then_inc(wo_hi, 1)

            def z_evacuate(i, odd):
                act.wait_ge(z_psum, i + 1)
                act.activation(z[0][:], psum[:, Z_BANK[1 - odd], :], ACT.Copy).then_inc(z_hi, 1)

            walk(act, step, lambda b: ht_evacuate(b + 1), lambda: None, lambda: z_evacuate(HEADS - 1, 1))

        @block.vector
        def _(dve):
            def layer_norm(b):
                dve.wait_ge(x_loaded, b * DMA_INC + DMA_INC)
                for t in range(NT):
                    dve.bn_stats(stats[:, t, :], xin[:, t, :]).then_inc(ln_chain, 1)
                alone(dve, ln_chain, b * 2 * NT + NT)
                for t in range(NT):
                    dve.bn_aggr(mv[:, t, :], stats[:, t, :]).then_inc(ln_chain, 1)
                dve.wait_ge(ln_chain, b * 2 * NT + 2 * NT)
                dve.tensor_scalar(mv[:, :, 1], mv[:, :, 1], LN_EPS, None, ALU.add).then_inc(ln_var, 1)
                dve.wait_ge(ln_rstd, b + 1)
                for t in range(NT):
                    last = dve.tensor_scalar(xin[:, t, :], xin[:, t, :], mv[:, t, 0:1], rstd[:, t:t + 1],
                                             ALU.subtract, ALU.mult)
                last.then_inc(ln_ready, 1)

            def ht_split_lo(b):
                dve.wait_ge(ht_hi, b + 1)
                dve.tensor_tensor(ht[1][:], ht32[:], ht[0][:], ALU.subtract).then_inc(ht_split, 1)

            def qk_lo(i, odd):
                for n, dst in enumerate((qt, kt)):
                    dve.wait_ge(qk_hi, i * 2 + n + 1)
                    dve.tensor_tensor(dst[1][:], psum[:, QK_BANK[1 - odd][n], :], dst[0][:],
                                      ALU.subtract).then_inc(qk_split, 1)

            def zero_acc():
                dve.memset(psum[:, ACC_BANK:ACC_BANK + 2, :], 0.0).then_inc(acc_zero, 1)

            dve.sem_inc(y_free, DMA_INC)
            dve.sem_inc(acc_gated, 1)
            layer_norm(0)
            dve.wait_ge(mod_psum, 1)
            for k in (0, 2):
                dve.tensor_copy(mod_t[:, k * DC:(k + 1) * DC, :],
                                psum[:, 0, k * DC * B:(k + 1) * DC * B].rearrange("p (k b) -> p k b", b=B))
            for k in (1, 3):
                last = dve.tensor_scalar(mod_t[:, k * DC:(k + 1) * DC, :],
                                         psum[:, 0, k * DC * B:(k + 1) * DC * B].rearrange("p (k b) -> p k b", b=B),
                                         1.0, None, ALU.add)
            last.then_inc(mod_ready, 1)
            ht_split_lo(0)
            dve.wait_ge(mod_psum, 2)
            dve.tensor_copy(gates8[:], psum[0:B, 1, :]).then_inc(g8, 1)
            dve.wait_ge(g8, 1)
            dve.tensor_scalar(gates8s[:], gates8[:], 0.0, 2.0, ALU.is_ge, ALU.mult).then_inc(g8, 1)
            dve.scalar_tensor_tensor(out=gates8a[:], in0=gates8[:], scalar=-1.0, in1=gates8[:],
                                     op0=ALU.mult, op1=ALU.max).then_inc(g8, 1)
            dve.wait_ge(g8, 3)
            dve.tensor_scalar(gates8a[:], gates8a[:], GATE_MIN, None, ALU.max).then_inc(g8, 1)
            dve.wait_ge(g8, 4)
            dve.scalar_tensor_tensor(out=gates8[:], in0=gates8s[:], scalar=-1.0, in1=gates8a[:],
                                     op0=ALU.add, op1=ALU.mult).then_inc(g8_ready, 1)
            dve.wait_ge(wqk_loaded, DMA_INC)
            wq = wqk[:, 0:H, 0:DC * P]
            dve.tensor_scalar(wq, wq, -SCALE, None, ALU.mult).then_inc(wq_scaled, 1)
            qk_lo(0, 0)
            dve.wait_ge(wv_hi, 1)
            dve.tensor_tensor(wv[1][:].rearrange("p a c n -> p (a c n)"), stage[:],
                              wv[0][:].rearrange("p a c n -> p (a c n)"), ALU.subtract).then_inc(wv_split, 1)

            def z_lo(i, odd):
                dve.wait_ge(z_hi, i + 1)
                dve.tensor_tensor(z[1][:], psum[:, Z_BANK[1 - odd], :], z[0][:], ALU.subtract).then_inc(z_split, 1)

            def gate_output(b):
                dve.wait_ge(o_done, b * H + H)
                dve.wait_ge(y_free, b * DMA_INC + DMA_INC)
                for k in range(2):
                    last = dve.tensor_tensor(
                        y[:, 2 * k:2 * k + 2, :], acc[:, 2 * k:2 * k + 2, :],
                        gates[:, bass.ds(b, 1), 0:D].to_broadcast([P, 2, D]), ALU.mult)
                last.then_inc(acc_gated, 1)

            def step(i, h, odd, b, pair=0, first=False, turn=False, new=False, last=False):
                if turn:
                    ht_split_lo(b + 1)
                for n, t in enumerate(S_ORDER):
                    alone(dve, s_psum, i * 3 + (1, 2, 2, 3)[n])
                    width = P * (t + 1)
                    dve.tensor_tensor_reduce(
                        out=probs[:, odd, tile_at(t):tile_at(t + 1)],
                        in0=psum[:, S_BANK[odd][t], S_COL[t]:S_COL[t] + width], in1=mask[:, SEQ - width:],
                        scale=1.0, scalar=HUGE, op0=ALU.add, op1=ALU.min,
                        accum_out=neg_max[:, odd, t:t + 1]).then_inc(s_masked, 1)
                if not first:
                    z_lo(i - 1, 1 - odd)
                dve.wait_ge(p_exp, i * NT + NT)
                dve.reciprocal(inv_sum[:, odd, :], row_sum[:, odd, :]).then_inc(sum_inv, 1)
                if not last:
                    qk_lo(i + 1, 1 - odd)
                if new:
                    gate_output(b - 1)
                if not odd:
                    for half in range(2):
                        dve.wait_ge(v_hi, i + half + 1)
                        out = v[1][:, 2 * half:2 * half + 2, :].rearrange("p t n -> p (t n)")
                        hi = v[0][:, 2 * half:2 * half + 2, :].rearrange("p t n -> p (t n)")
                        dve.tensor_tensor(out, psum[:, V_BANK[half], :], hi, ALU.subtract).then_inc(v_split, 1)
                for n in range(3):
                    dve.wait_ge(t_hi, i * 3 + n + 1)
                    at = slice(n * 4 * P, n * 4 * P + T_WIDTH[n])
                    dve.tensor_tensor(pt[1][:, at], psum[:, T_BANK[odd][n], 0:T_WIDTH[n]], pt[0][:, at],
                                      ALU.subtract).then_inc(t_split, 1)
                if first:
                    dve.wait_ge(wo_hi, 1)
                    dve.tensor_tensor(wo[1][:].rearrange("p a n -> p (a n)"), stage[:],
                                      wo[0][:].rearrange("p a n -> p (a n)"), ALU.subtract).then_inc(wo_split, 1)

            def batch_begin(b):
                layer_norm(b + 1)
                dve.wait_ge(ht32_ready, b * DC + 2 * DC)
                zero_acc()

            def tail():
                z_lo(HEADS - 1, 1)
                gate_output(B - 1)

            def last_begin():
                dve.wait_ge(acc_gated, B)
                zero_acc()

            walk(dve, step, batch_begin, last_begin, tail)

        @block.tensor
        def _(pe):
            def split_product(out, stationary, moving, start, stop, skip=False):
                for n, (s, m) in enumerate(PASSES):
                    last = pe.matmul(out, stationary(s), moving(m), start=start and n == 0,
                                     stop=stop and n == len(PASSES) - 1, skip_group_check=skip)
                return last

            def layer_norm_transposes(b):
                pe.wait_ge(ln_ready, b + 1)
                for c in range(DC):
                    for t in range(NT):
                        last = pe.transpose(psum[:, ACC_BANK + c, t * P:(t + 1) * P],
                                            xin[:, t, c * P:(c + 1) * P], ident[:])
                    last.then_inc(ln_psum, 1)

            def queries_keys(i, odd):
                pe.wait_ge(w_staged, i + 1)
                for n in range(2):
                    for c in range(DC):
                        last = split_product(psum[:, QK_BANK[1 - odd][n], :], lambda s: ws[s][:, n, c, :],
                                             lambda m: ht[m][:, c, :], c == 0, c == DC - 1)
                    last.then_inc(qk_psum, 1)

            pe.wait_ge(c_act, 1)
            pe.wait_ge(wmod_loaded, DMA_INC)
            for k, first_col in enumerate((0, D, 3 * D, 4 * D)):
                for j in range(DC):
                    col = first_col + j * P
                    at = (k * DC + j) * B
                    for c in range(DC):
                        last = pe.matmul(psum[:, 0, at:at + B], wmod[:, c, col:col + P], act_c[:, c, :],
                                         start=(c == 0), stop=(c == DC - 1))
            last.then_inc(mod_psum, 1)
            for k in range(2):
                for c in range(DC):
                    last = pe.matmul(psum[0:B, 1, k * D:(k + 1) * D], act_c[:, c, :],
                                     wmod[:, c, (3 * k + 2) * D:(3 * k + 3) * D], start=(c == 0), stop=(c == DC - 1))
            last.then_inc(mod_psum, 1)
            pe.wait_ge(consts, 7)
            layer_norm_transposes(0)
            pe.wait_ge(ht_split, 1)
            queries_keys(0, 0)
            pe.wait_ge(g8_ready, 1)
            for b in range(B):
                if b >= 3:
                    pe.wait_ge(gate_copied, b - 2)
                pe.matmul(psum[:, 3 + b % 3, :], pick[:, b, :], gates8[:], start=True, stop=True).then_inc(gate_psum, 1)

            def scores(i, odd):
                pe.wait_ge(qk_split, i * 2 + 2)
                for n, t in enumerate(S_ORDER):
                    if t == 3:
                        if odd:
                            pe.wait_ge(v_split, i + 1)
                    width = P * (t + 1)
                    last = split_product(psum[:, S_BANK[odd][t], S_COL[t]:S_COL[t] + width],
                                         lambda s: qt[s][:, t * P:(t + 1) * P], lambda m: kt[m][:, 0:width],
                                         True, True)
                    if t != 0:
                        last.then_inc(s_psum, 1)

            def weighted_values(i, odd):
                pe.wait_ge(t_split, i * 3 + 3)
                for j in range(NT):
                    width = SEQ - P * j
                    last = split_product(psum[:, Z_BANK[1 - odd], P * j:], lambda s: v[s][:, j, odd * P:(odd + 1) * P],
                                         lambda m: pt[m][:, PT_AT[j]:PT_AT[j] + width], j == 0, j == NT - 1)
                last.then_inc(z_psum, 1)

            def project(i, h):
                pe.wait_ge(z_split, i + 1)
                for t in range(NT):
                    last = split_product(acc[:, t, :], lambda s: z[s][:, t * P:(t + 1) * P],
                                         lambda m: wo[m][:, h, :], False, True, skip=True)
                last.then_inc(o_done, 1)

            def values(i, pair):
                pe.wait_ge(s_masked, i * NT + 1)
                for t in range(NT):
                    for c in range(DC):
                        last = split_product(psum[:, V_BANK[t // 2], (t % 2) * 2 * P:(t % 2 + 1) * 2 * P],
                                             lambda s: ht[s][:, c, t * P:(t + 1) * P],
                                             lambda m: wv[m][:, pair, c, :], c == 0, c == DC - 1)
                    if t % 2:
                        last.then_inc(v_psum, 1)

            def transposes(i, odd):
                pe.wait_ge(p_norm, i * NT + NT)
                for n, held in enumerate(T_HOLDS):
                    if n == 2 and not odd:
                        pe.wait_ge(v_split, i + 1)
                    for j, col in held:
                        for t in range(j, NT):
                            last = pe.transpose(psum[:, T_BANK[odd][n], col + (t - j) * P:col + (t - j + 1) * P],
                                                probs[:, odd, tile_at(t) + j * P:tile_at(t) + (j + 1) * P], ident[:])
                    last.then_inc(t_psum, 1)

            def step(i, h, odd, b, pair=0, first=False, turn=False, new=False, last=False):
                scores(i, odd)
                if not first:
                    weighted_values(i - 1, 1 - odd)
                if turn:
                    pe.wait_ge(ht_split, b + 2)
                if first:
                    pe.wait_ge(gate_copied, B)
                if not last:
                    queries_keys(i + 1, 1 - odd)
                if not first:
                    if not new:
                        pe.wait_ge(acc_zero, b + 1)
                    project(i - 1, H - 1 if new else h - 1)
                if not odd:
                    if first:
                        pe.wait_ge(wv_split, 1)
                    values(i, pair)
                transposes(i, odd)
                if first:
                    pe.wait_ge(wo_split, 1)

            def batch_begin(b):
                pe.wait_ge(acc_gated, b + 1)
                layer_norm_transposes(b + 1)

            def tail():
                weighted_values(HEADS - 1, 1)
                project(HEADS - 1, H - 1)

            walk(pe, step, batch_begin, lambda: None, tail)


def feed_forward_layer(nc, psum, stage, mod_t, gates, ident, x1, up_loaded, down_d, wg_d, bg_d, bgate_d, bup_d,
                       bsup_d, bdown_d, bsdown_d, out):
    B, SEQ, D = x1.shape
    NT = SEQ // P
    DC = D // P
    NE = bgate_d.shape[1]
    NS = bsup_d.shape[1]
    NG = wg_d.shape[2]
    KEPT = NE
    UPS = NS + 2 * NE
    UP, HID, DOWN = NS + 2 * NE, NS + NE, NE + 1
    Y_BANK = (4, 6)
    LOGIT_T_BANK, LOGIT_BANK = 2, 3

    with ExitStack() as ctx:
        def sb(name, shape, dt=F32):
            return ctx.enter_context(nc.sbuf_tensor(name, shape, dt))

        def sem(name):
            return ctx.enter_context(nc.semaphore(name))

        def pair_of(name, shape):
            return [sb(name + "_hi", shape, F32R), sb(name + "_lo", shape, F32R)]

        up = pair_of("f_up", [P, UPS, DC, P])
        down_raw = sb("f_down_raw", [P, NE + NS, D])
        down = pair_of("f_down", [P, NE + NS, D])
        wg = sb("f_wg", [P, DC, NG])
        bg = sb("f_bg", [NG, 1])
        b_gate = sb("f_b_gate", [P, NE])
        b_up = sb("f_b_up", [P, NE])
        b_sup = sb("f_b_sup", [P, NS])
        b_out = sb("f_b_out", [NE + 1, D])
        minus_half = sb("f_minus_half", [P, NT])
        earlier = sb("f_earlier", [P, NG, NG])
        xin = sb("f_xin", [P, NT, D])
        stats = sb("f_stats", [P, NT, 6])
        mv = sb("f_mv", [P, NT, 2])
        rstd = sb("f_rstd", [P, NT])
        ht32 = sb("f_ht32", [P, DC, SEQ])
        ht = pair_of("f_ht", [P, DC, SEQ])
        logit_t = sb("f_logit_t", [NG, SEQ])
        logit = sb("f_logit", [P, NT, NG])
        top = sb("f_top", [P, NT])
        above = sb("f_above", [P, NT, NG, NG])
        equal = sb("f_equal", [P, NT, NG, NG])
        rank = sb("f_rank", [P, NT, NG])
        kept = sb("f_kept", [P, NT, NG])
        shifted = sb("f_shifted", [P, NT, NG])
        weight = sb("f_weight", [P, NT, NG])
        total = sb("f_total", [P, NT])
        inv_total = sb("f_inv_total", [P, NT])
        weight1 = sb("f_weight1", [P, NT, NE + 1])
        weight_t = sb("f_weight_t", [NE + 1, SEQ])
        gated = sb("f_gated", [P, 2, SEQ])
        hid32 = sb("f_hid32", [P, 2, SEQ])
        hid = [pair_of(f"f_hid{n}", [P, SEQ]) for n in range(2)]
        shid32 = sb("f_shid32", [P, NS, SEQ])
        shid = [pair_of(f"f_shid{n}", [P, SEQ]) for n in range(NS)]
        f = sb("f_sum", [P, NT, D])
        xres = sb("f_xres", [P, NT, D])
        y = sb("f_y", [P, NT, D])

        down_loaded = sem("f_down_loaded")
        small_loaded = sem("f_small_loaded")
        x_loaded = sem("f_x_loaded")
        xres_loaded = sem("f_xres_loaded")
        y_free = sem("f_y_free")
        consts = sem("f_consts")
        up_hi = sem("f_up_hi")
        up_split = sem("f_up_split")
        down_hi = sem("f_down_hi")
        down_split = sem("f_down_split")
        ln_chain = sem("f_ln_chain")
        ln_var = sem("f_ln_var")
        ln_rstd = sem("f_ln_rstd")
        ln_ready = sem("f_ln_ready")
        ln_psum = sem("f_ln_psum")
        ht32_ready = sem("f_ht32_ready")
        ht_hi = sem("f_ht_hi")
        ht_split = sem("f_ht_split")
        logit_t_psum = sem("f_logit_t_psum")
        logit_t_ready = sem("f_logit_t_ready")
        logit_psum = sem("f_logit_psum")
        route = sem("f_route")
        shifted_ready = sem("f_shifted_ready")
        weight_exp = sem("f_weight_exp")
        weight_ready = sem("f_weight_ready")
        weight_t_psum = sem("f_weight_t_psum")
        weight_t_ready = sem("f_weight_t_ready")
        up_psum = sem("f_up_psum")
        silu_done = sem("f_silu_done")
        glu_done = sem("f_glu_done")
        hid_hi = sem("f_hid_hi")
        hid_split = sem("f_hid_split")
        down_psum = sem("f_down_psum")
        summed = sem("f_summed")
        f_read = sem("f_f_read")
        y_ready = sem("f_y_ready")

        def y_bank(k):
            return psum[:, Y_BANK[k]:Y_BANK[k] + 2, :].rearrange("p k (t n) -> p (k t) n", t=2)

        block = ctx.enter_context(nc.Block())

        @block.sync
        def _(sp):
            sp.dma_start(xin[:], rows(x1, 0)).then_inc(x_loaded, DMA_INC)
            sp.dma_start(down_raw[:].rearrange("p a n -> p (a n)"), down_d).then_inc(down_loaded, DMA_INC)
            for dst, src in ((wg, wg_d), (bg, bg_d), (b_gate, bgate_d), (b_up, bup_d), (b_sup, bsup_d)):
                sp.dma_start(dst[:], src).then_inc(small_loaded, DMA_INC)
            sp.dma_start(b_out[0:NE, :], bdown_d).then_inc(small_loaded, DMA_INC)
            sp.dma_start(b_out[NE:NE + 1, :], bsdown_d).then_inc(small_loaded, DMA_INC)
            with sp.Fori(0, B - 1) as b:
                sp.wait_ge(ln_psum, b * DC + DC)
                sp.dma_start(xin[:], rows(x1, b + 1)).then_inc(x_loaded, DMA_INC)
                sp.dma_start(xres[:], rows(x1, b)).then_inc(xres_loaded, DMA_INC)
                sp.wait_ge(y_ready, b + 1)
                sp.dma_start(rows(out, b), y[:]).then_inc(y_free, DMA_INC)
            sp.dma_start(xres[:], rows(x1, B - 1)).then_inc(xres_loaded, DMA_INC)
            sp.wait_ge(y_ready, B)
            sp.dma_start(rows(out, B - 1), y[:]).then_inc(y_free, DMA_INC)
            sp.wait_ge(y_free, B * DMA_INC + DMA_INC)

        @block.gpsimd
        def _(pool):
            pool.memset(minus_half[:], -0.5).then_inc(consts, 1)
            pool.memset(earlier[:], 1.0).then_inc(consts, 1)
            pool.memset(weight1[:], 1.0).then_inc(consts, 1)
            pool.wait_ge(consts, 3)
            pool.affine_select(out=earlier[:], in_=earlier[:], compare_op=ALU.is_ge, fill=0.0, base=-1,
                               pattern=[[1, NG], [-1, NG]], channel_multiplier=0).then_inc(consts, 1)

            def layer_norm_rstd(b):
                pool.wait_ge(ln_var, b + 1)
                pool.tensor_tensor(rstd[:], mv[:, :, 1], minus_half[:], ALU.pow).then_inc(ln_rstd, 1)

            def finish(b):
                pool.wait_ge(summed, b * DOWN + DOWN + 1)
                alone(pool, y_free, b * DMA_INC + DMA_INC)
                gate = gates[:, bass.ds(b, 1), D:2 * D].to_broadcast([P, NT, D])
                pool.tensor_tensor(y[:], f[:], gate, ALU.mult).then_inc(f_read, 1)
                pool.wait_ge(xres_loaded, b * DMA_INC + DMA_INC)
                alone(pool, f_read, b + 2)
                pool.tensor_tensor(y[:], y[:], xres[:], ALU.add).then_inc(y_ready, 1)

            layer_norm_rstd(0)
            with pool.Fori(0, B - 1) as b:
                layer_norm_rstd(b + 1)
                finish(b)
            finish(B - 1)

        @block.scalar
        def _(act):
            def ht_evacuate(b):
                for c in range(DC):
                    act.wait_ge(ln_psum, b * DC + c + 1)
                    act.activation(ht32[:, c, :], psum[:, Y_BANK[0] + c, :], ACT.Identity,
                                   bias=mod_t[:, 2 * DC + c, bass.ds(b, 1)],
                                   scale=mod_t[:, 3 * DC + c, bass.ds(b, 1)]).then_inc(ht32_ready, 1)

            def ht_split_hi(b):
                act.wait_ge(ht32_ready, b * DC + DC)
                act.activation(ht[0][:], ht32[:], ACT.Copy).then_inc(ht_hi, 1)

            act.wait_ge(up_loaded, DMA_INC)
            act.activation(up[0][:].rearrange("p a c n -> p (a c n)"), stage[:, 0:UPS * DC * P],
                           ACT.Copy).then_inc(up_hi, 1)
            ht_evacuate(0)
            ht_split_hi(0)
            act.wait_ge(down_loaded, DMA_INC)
            act.activation(down[0][:], down_raw[:], ACT.Copy).then_inc(down_hi, 1)
            act.wait_ge(small_loaded, 7 * DMA_INC)

            def hi(b, n, dst, src):
                act.activation(dst[0][:], src, ACT.Copy).then_inc(hid_hi, 1)

            def batch(b, last=False):
                act.wait_ge(logit_t_psum, b + 1)
                act.activation(logit_t[:], psum[0:NG, LOGIT_T_BANK, :], ACT.Identity,
                               bias=bg[:]).then_inc(logit_t_ready, 1)
                for m in range(NS):
                    act.wait_ge(up_psum, b * UP + m + 1)
                    act.activation(shid32[:, m, :], psum[:, m, :], ACT.Silu,
                                   bias=b_sup[:, m:m + 1]).then_inc(silu_done, 1)
                    act.wait_ge(silu_done, b * HID + m + 1)
                    hi(b, m, shid[m], shid32[:, m, :])
                act.wait_ge(shifted_ready, b + 1)
                act.activation(weight[:], shifted[:], ACT.Exp).then_inc(weight_exp, 1)
                for n in range(NE):
                    act.wait_ge(up_psum, b * UP + NS + 2 * n + 1)
                    act.activation(gated[:, n % 2, :], psum[:, n % 2, :], ACT.Silu,
                                   bias=b_gate[:, n:n + 1]).then_inc(silu_done, 1)
                    if n == 0:
                        act.wait_ge(weight_t_psum, b + 1)
                        act.activation(weight_t[:], psum[0:NE + 1, LOGIT_BANK, :], ACT.Copy).then_inc(weight_t_ready, 1)
                    act.wait_ge(glu_done, b * NE + n + 1)
                    hi(b, NS + n, hid[n % 2], hid32[:, n % 2, :])
                    if n == NE - 2 and not last:
                        ht_evacuate(b + 1)
                if not last:
                    act.wait_ge(up_psum, b * UP + UP)
                    ht_split_hi(b + 1)

            with act.Fori(0, B - 1) as b:
                batch(b)
            batch(B - 1, last=True)

        @block.vector
        def _(dve):
            def layer_norm(b):
                dve.wait_ge(x_loaded, b * DMA_INC + DMA_INC)
                for t in range(NT):
                    dve.bn_stats(stats[:, t, :], xin[:, t, :]).then_inc(ln_chain, 1)
                alone(dve, ln_chain, b * 2 * NT + NT)
                for t in range(NT):
                    dve.bn_aggr(mv[:, t, :], stats[:, t, :]).then_inc(ln_chain, 1)
                dve.wait_ge(ln_chain, b * 2 * NT + 2 * NT)
                dve.tensor_scalar(mv[:, :, 1], mv[:, :, 1], LN_EPS, None, ALU.add).then_inc(ln_var, 1)
                dve.wait_ge(ln_rstd, b + 1)
                for t in range(NT):
                    last = dve.tensor_scalar(xin[:, t, :], xin[:, t, :], mv[:, t, 0:1], rstd[:, t:t + 1],
                                             ALU.subtract, ALU.mult)
                last.then_inc(ln_ready, 1)

            def ht_split_lo(b):
                dve.wait_ge(ht_hi, b + 1)
                dve.tensor_tensor(ht[1][:], ht32[:], ht[0][:], ALU.subtract).then_inc(ht_split, 1)

            dve.sem_inc(y_free, DMA_INC)
            dve.sem_inc(summed, 1)
            dve.sem_inc(f_read, 1)
            layer_norm(0)
            dve.wait_ge(up_hi, 1)
            dve.tensor_tensor(up[1][:].rearrange("p a c n -> p (a c n)"), stage[:, 0:UPS * DC * P],
                              up[0][:].rearrange("p a c n -> p (a c n)"), ALU.subtract).then_inc(up_split, 1)
            ht_split_lo(0)
            dve.wait_ge(down_hi, 1)
            dve.tensor_tensor(down[1][:], down_raw[:], down[0][:], ALU.subtract).then_inc(down_split, 1)
            dve.wait_ge(consts, 4)

            def lo(b, n, dst, src):
                dve.wait_ge(hid_hi, b * HID + n + 1)
                dve.tensor_tensor(dst[1][:], src, dst[0][:], ALU.subtract).then_inc(hid_split, 1)

            ROUTE = 9

            def ranks(b):
                dve.wait_ge(logit_psum, b + 1)
                dve.tensor_copy(logit[:].rearrange("p t n -> p (t n)"), psum[:, LOGIT_BANK, 0:NT * NG]).then_inc(route, 1)
                dve.wait_ge(route, b * ROUTE + 1)
                by_j = logit[:].rearrange("p t (i n) -> p t i n", i=1).to_broadcast([P, NT, NG, NG])
                by_i = logit[:].rearrange("p t (n i) -> p t n i", i=1).to_broadcast([P, NT, NG, NG])
                dve.tensor_tensor(above[:], by_j, by_i, ALU.is_gt).then_inc(route, 1)
                dve.tensor_tensor(equal[:], by_j, by_i, ALU.is_equal).then_inc(route, 1)
                dve.tensor_reduce(top[:], logit[:], AX_X, ALU.max).then_inc(route, 1)
                dve.wait_ge(route, b * ROUTE + 4)
                dve.tensor_tensor(shifted[:], logit[:], top[:].rearrange("p (t i) -> p t i", i=1).to_broadcast([P, NT, NG]),
                                  ALU.subtract).then_inc(shifted_ready, 1)
                for t in range(NT):
                    last = dve.tensor_tensor(equal[:, t, :, :], equal[:, t, :, :], earlier[:], ALU.mult)
                last.then_inc(route, 1)
                dve.wait_ge(route, b * ROUTE + 5)
                dve.tensor_tensor(above[:], above[:], equal[:], ALU.add).then_inc(route, 1)
                dve.wait_ge(route, b * ROUTE + 6)
                dve.tensor_reduce(rank[:], above[:], AX_X, ALU.add).then_inc(route, 1)

            def weights(b):
                dve.wait_ge(route, b * ROUTE + 7)
                dve.wait_ge(weight_exp, b + 1)
                dve.scalar_tensor_tensor(out=kept[:], in0=rank[:], scalar=float(KEPT), in1=weight[:],
                                         op0=ALU.is_lt, op1=ALU.mult).then_inc(route, 1)
                dve.wait_ge(route, b * ROUTE + 8)
                dve.tensor_reduce(total[:], kept[:], AX_X, ALU.add).then_inc(route, 1)
                dve.wait_ge(route, b * ROUTE + 9)
                dve.reciprocal(inv_total[:], total[:]).then_inc(weight_ready, 1)
                dve.wait_ge(weight_ready, b * 2 + 1)
                dve.tensor_tensor(weight1[:, :, 0:NE], kept[:, :, 0:NE],
                                  inv_total[:].rearrange("p (t i) -> p t i", i=1).to_broadcast([P, NT, NE]),
                                  ALU.mult).then_inc(weight_ready, 1)

            def glu(b, n):
                dve.wait_ge(up_psum, b * UP + NS + 2 * n + 2)
                dve.wait_ge(silu_done, b * HID + NS + n + 1)
                dve.scalar_tensor_tensor(out=hid32[:, n % 2, :], in0=psum[:, 2 + n % 2, :], scalar=b_up[:, n:n + 1],
                                         in1=gated[:, n % 2, :], op0=ALU.add, op1=ALU.mult).then_inc(glu_done, 1)

            def add_expert(b, n):
                if n == 0:
                    dve.wait_ge(f_read, b + 1)
                    dve.wait_ge(weight_ready, b * 2 + 2)
                dve.wait_ge(down_psum, b * DOWN + (n + 1 if n < NE - 1 else DOWN))
                src = y_bank(n % 2 if n < NE - 2 else 1)
                for t in range(NT):
                    w = weight1[:, t, n:n + 1]
                    if n == 0:
                        last = dve.tensor_scalar(f[:, t, :], src[:, t, :], w, None, ALU.mult)
                    else:
                        last = dve.scalar_tensor_tensor(out=f[:, t, :], in0=src[:, t, :], scalar=w, in1=f[:, t, :],
                                                        op0=ALU.mult, op1=ALU.add)
                last.then_inc(summed, 1)

            def add_shared(b):
                dve.wait_ge(down_psum, b * DOWN + DOWN - 1)
                for k in range(2):
                    last = dve.tensor_tensor(f[:, 2 * k:2 * k + 2, :], y_bank(0)[:, 2 * k:2 * k + 2, :],
                                             f[:, 2 * k:2 * k + 2, :], ALU.add)
                last.then_inc(summed, 1)

            def batch(b, last=False):
                lo(b, 0, shid[0], shid32[:, 0, :])
                ranks(b)
                lo(b, 1, shid[1], shid32[:, 1, :])
                weights(b)
                for n in range(NE):
                    glu(b, n)
                    if n == 2 and not last:
                        layer_norm(b + 1)
                    lo(b, NS + n, hid[n % 2], hid32[:, n % 2, :])
                    if n >= 1:
                        dve.wait_ge(summed, b * DOWN + n)
                        add_expert(b, n - 1)
                if not last:
                    ht_split_lo(b + 1)
                dve.wait_ge(summed, b * DOWN + NE)
                add_shared(b)
                dve.wait_ge(summed, b * DOWN + NE + 1)
                add_expert(b, NE - 1)

            with dve.Fori(0, B - 1) as b:
                batch(b)
            batch(B - 1, last=True)

        @block.tensor
        def _(pe):
            def split_product(out, stationary, moving, start, stop):
                for n, (s, m) in enumerate(PASSES):
                    last = pe.matmul(out, stationary(s), moving(m), start=start and n == 0,
                                     stop=stop and n == len(PASSES) - 1)
                return last

            def layer_norm_transposes(b):
                pe.wait_ge(ln_ready, b + 1)
                for c in range(DC):
                    for t in range(NT):
                        last = pe.transpose(psum[:, Y_BANK[0] + c, t * P:(t + 1) * P],
                                            xin[:, t, c * P:(c + 1) * P], ident[:])
                    last.then_inc(ln_psum, 1)

            def up_product(k, bank):
                for c in range(DC):
                    last = split_product(psum[:, bank, :], lambda s: up[s][:, k, c, :], lambda m: ht[m][:, c, :],
                                         c == 0, c == DC - 1)
                last.then_inc(up_psum, 1)

            def down_product(b, n):
                pe.wait_ge(hid_split, b * HID + NS + n + 1)
                dst = y_bank(n % 2 if n < NE - 2 else 1)
                for t in range(NT):
                    last = split_product(dst[:, t, :], lambda s: hid[n % 2][s][:, t * P:(t + 1) * P],
                                         lambda m: down[m][:, n, :], True, True)
                last.then_inc(down_psum, 1)

            def shared_down_product(b):
                pe.wait_ge(hid_split, b * HID + NS)
                pe.wait_ge(weight_t_ready, b + 1)
                for t in range(NT):
                    dst = y_bank(0)[:, t, :]
                    for m in range(NS):
                        split_product(dst, lambda s: shid[m][s][:, t * P:(t + 1) * P],
                                      lambda k: down[k][:, NE + m, :], m == 0, False)
                    last = pe.matmul(dst, weight_t[:, t * P:(t + 1) * P], b_out[:], start=False, stop=True)
                last.then_inc(down_psum, 1)

            def batch(b, last=False):
                for c in range(DC):
                    mm = pe.matmul(psum[0:NG, LOGIT_T_BANK, :], wg[:, c, :], ht32[:, c, :],
                                   start=(c == 0), stop=(c == DC - 1))
                mm.then_inc(logit_t_psum, 1)
                pe.wait_ge(ht_split, b + 1)
                up_product(0, 0)
                alone(pe, logit_t_ready, b + 1)
                for t in range(NT):
                    mm = pe.transpose(psum[:, LOGIT_BANK, t * NG:(t + 1) * NG], logit_t[:, t * P:(t + 1) * P],
                                      ident[0:NG, 0:NG])
                mm.then_inc(logit_psum, 1)
                up_product(1, 1)
                for n in range(NE):
                    if n < 2:
                        pe.wait_ge(silu_done, b * HID + n + 1)
                    up_product(NS + 2 * n, n % 2)
                    up_product(NS + 2 * n + 1, 2 + n % 2)
                    if n == 0:
                        pe.wait_ge(weight_ready, b * 2 + 2)
                        for t in range(NT):
                            mm = pe.transpose(psum[0:NE + 1, LOGIT_BANK, t * P:(t + 1) * P], weight1[:, t, :], ident[:])
                        mm.then_inc(weight_t_psum, 1)
                        pe.wait_ge(weight_t_ready, b + 1)
                    if n >= 1:
                        if n == 1:
                            pe.wait_ge(summed, b * DOWN + 1)
                        if n >= 3:
                            pe.wait_ge(summed, b * DOWN + (n if n == NE - 1 else n - 1))
                        down_product(b, n - 1)
                    if n == NE - 2 and not last:
                        pe.wait_ge(summed, b * DOWN + 4)
                        layer_norm_transposes(b + 1)
                if last:
                    pe.wait_ge(summed, b * DOWN + 4)
                else:
                    pe.wait_ge(ht32_ready, b * DC + 2 * DC)
                shared_down_product(b)
                pe.wait_ge(summed, b * DOWN + NE)
                down_product(b, NE - 1)

            layer_norm_transposes(0)
            pe.wait_ge(up_split, 1)
            pe.wait_ge(ht32_ready, DC)
            pe.wait_ge(small_loaded, 7 * DMA_INC)
            pe.wait_ge(down_split, 1)
            pe.wait_ge(consts, 4)
            with pe.Fori(0, B - 1) as b:
                batch(b)
            batch(B - 1, last=True)


def adaln_block(nc, x, wqk_d, wv_d, wo_d, c_d, wmod_d, up_d, down_d, wg_d, bg_d, bgate_d, bup_d, bsup_d, bdown_d,
                bsdown_d, out):
    B, SEQ, D = x.shape
    x1 = nc.dram_tensor("x1_dram", [B, SEQ, D], F32).ap()
    with ExitStack() as ctx:
        def sb(name, shape):
            return ctx.enter_context(nc.sbuf_tensor(name, shape, F32))

        psum = ctx.enter_context(nc.psum_tensor("psum", [P, 8, 512], F32))
        stage = sb("stage", [P, wo_d.shape[1]])
        mod_t = sb("mod_t", [P, 4 * D // P, B])
        gates = sb("gates", [P, B, 2 * D])
        ident = sb("ident", [P, P])
        up_loaded = ctx.enter_context(nc.semaphore("up_loaded"))
        shared = (nc, psum, stage, mod_t, gates, ident)
        attention_layer(*shared, x, wqk_d, wv_d, wo_d, c_d, wmod_d, up_d, up_loaded, x1)
        feed_forward_layer(*shared, x1, up_loaded, down_d, wg_d, bg_d, bgate_d, bup_d, bsup_d, bdown_d, bsdown_d, out)


def kernel(**inputs):
    import numpy as np
    import concourse.bacc as bacc
    from concourse.bass_utils import run_bass_kernel_spmd

    def get(name):
        return np.asarray(inputs["L0_" + name])

    x = get("attn_x")
    B, SEQ, D = x.shape
    H, E, _ = get("attn_W_Q").shape
    DC = D // P
    NE, _, HID = get("ffn_Wgate").shape
    NS = get("ffn_Ws_up").shape[1] // P

    def qk_layout(w):
        return w.reshape(H, E, DC, P).transpose(3, 0, 2, 1)

    def up_layout(w, n):
        return w.reshape(n, DC, P, HID).transpose(2, 0, 1, 3)

    experts = np.stack([up_layout(get("ffn_Wgate"), NE), up_layout(get("ffn_Wup"), NE)], 2)
    shared = get("ffn_Ws_up").reshape(DC, P, NS, HID).transpose(1, 2, 0, 3)
    arrays = {
        "x": x,
        "wqk": np.stack([qk_layout(get("attn_W_Q")), qk_layout(get("attn_W_K"))], 2).reshape(P, H, 2 * DC * E),
        "wv": get("attn_W_V").reshape(H // 2, 2, E, DC, P).transpose(4, 0, 3, 1, 2).reshape(P, H * DC * E),
        "wo": get("attn_W_O").transpose(2, 0, 1).reshape(P, H * D),
        "c": get("c").reshape(B, DC, P).transpose(2, 1, 0),
        "wmod": get("wmod").reshape(DC, P, 6 * D).transpose(1, 0, 2).reshape(P, DC * 6 * D),
        "up": np.concatenate([shared.reshape(P, -1), experts.reshape(P, -1)], 1),
        "down": np.concatenate([get("ffn_Wdown").transpose(1, 0, 2).reshape(P, -1),
                                get("ffn_Ws_down").reshape(NS, P, D).transpose(1, 0, 2).reshape(P, -1)], 1),
        "wg": get("ffn_Wg").reshape(DC, P, -1).transpose(1, 0, 2),
        "bg": get("ffn_bg").reshape(-1, 1),
        "bgate": get("ffn_bgate").transpose(1, 0),
        "bup": get("ffn_bup").transpose(1, 0),
        "bsup": get("ffn_bs_up").reshape(NS, P).transpose(1, 0),
        "bdown": get("ffn_bdown"),
        "bsdown": get("ffn_bs_down").reshape(1, D),
    }
    nc = bacc.Bacc("TRN2", target_bir_lowering=False, num_devices=1)
    launch, args = {}, []
    for name, a in arrays.items():
        a = np.ascontiguousarray(a)
        launch[f"in_{name}"] = a
        args.append(nc.dram_tensor(f"in_{name}", a.shape, mybir.dt.from_np(a.dtype), kind="ExternalInput").ap())
    args.append(nc.dram_tensor("block_out", x.shape, F32, kind="ExternalOutput").ap())
    adaln_block(nc, *args)
    r = run_bass_kernel_spmd(nc, [launch], core_ids=[0])
    return r.results[0]["block_out"]
```

```python
from contextlib import ExitStack

import concourse.bass as bass
from concourse import mybir

ALU = mybir.AluOpType
ACT = mybir.ActivationFunctionType
AX_X = mybir.AxisListType.X
F32 = mybir.dt.float32
F32R = mybir.dt.float32r

P = 128
DMA_INC = 16
LN_EPS = 1e-5
GATE_MIN = 0.25
MASKED = 1e30
HUGE = 3e38
PASSES = ((0, 0), (0, 1), (1, 0))

S_BANK = ({1: 0, 0: 2, 2: 2, 3: 1}, {1: 4, 0: 5, 2: 5, 3: 3})
S_COL = {1: 0, 0: 0, 2: P, 3: 0}
S_ORDER = (1, 0, 2, 3)
Z_BANK = (3, 1)
QK_BANK = ((4, 5), (0, 2))
V_BANK = (0, 3)
T_BANK = ((1, 2, 0), (3, 4, 5))
ACC_BANK = 6
T_HOLDS = (((0, 0),), ((1, 0), (3, 3 * P)), ((2, 0),))
T_WIDTH = (4 * P, 4 * P, 2 * P)
J_ORDER = (0, 1, 3, 2)
PT_AT = {0: 0, 1: 4 * P, 3: 7 * P, 2: 8 * P}


def tile_at(i):
    return P * (i * (i + 1) // 2)


def alone(eng, semaphore, value):
    eng.wait_ge(semaphore, value)
    eng.nop(nofuse=True)


def rows(dram, b):
    return dram[b].rearrange("(t p) d -> p t d", p=P)


def attention_layer(nc, psum, stage, mod_t, gates, ident, x, wqk_d, wv_d, wo_d, c_d, wmod_d, up_d, up_loaded, x1):
    B, SEQ, D = x.shape
    H = wo_d.shape[1] // D
    NT = SEQ // P
    DC = D // P
    PAIRS = H // 2
    SW = tile_at(NT)
    HEADS = B * H
    SCALE = 1.0 / float(P) ** 0.5
    CHUNKS = 4
    CHUNK = H * D // CHUNKS

    with ExitStack() as ctx:
        def sb(name, shape, dt=F32):
            return ctx.enter_context(nc.sbuf_tensor(name, shape, dt))

        def sem(name):
            return ctx.enter_context(nc.semaphore(name))

        def pair_of(name, shape):
            return [sb(name + "_hi", shape, F32R), sb(name + "_lo", shape, F32R)]

        wqk = sb("wqk", [P, H + 1, 2 * DC * P])
        wv = pair_of("wv", [P, PAIRS, DC, 2 * P])
        wo = pair_of("wo", [P, H, D])
        ws = pair_of("ws", [P, 2, DC, P])
        xin = sb("xin", [P, NT, D])
        ht32 = sb("ht32", [P, DC, SEQ])
        ht = pair_of("ht", [P, DC, SEQ])
        stats = sb("stats", [P, NT, 6])
        mv = sb("mv", [P, NT, 2])
        rstd = sb("rstd", [P, NT])
        minus_half = sb("minus_half", [P, NT])
        qt = pair_of("qt", [P, SEQ])
        kt = pair_of("kt", [P, SEQ])
        v = pair_of("v", [P, NT, 2 * P])
        probs = sb("probs", [P, 2, SW])
        pt = pair_of("pt", [P, SW])
        z = pair_of("z", [P, SEQ])
        neg_max = sb("neg_max", [P, 2, NT])
        row_sum = sb("row_sum", [P, 2, NT])
        inv_sum = sb("inv_sum", [P, 2, NT])
        xres = sb("xres", [P, NT, D])
        y = sb("y", [P, NT, D])
        act_c = sb("act_c", [P, DC, B])
        gates8 = sb("gates8", [B, 2 * D])
        gates8s = y[0:B, 0:2, :].rearrange("b t n -> b (t n)")
        gates8a = y[0:B, 2:4, :].rearrange("b t n -> b (t n)")
        mask = sb("mask", [P, SEQ])
        wmod = gates[:].rearrange("p b n -> p (b n)")[:, 0:DC * 6 * D].rearrange("p (c n) -> p c n", c=DC)
        wmod_v = wmod_d.rearrange("p (c n) -> p c n", c=DC)
        gates8_parts = [part[0:B, :] for part in z]

        c_loaded = sem("c_loaded")
        wmod_loaded = sem("wmod_loaded")
        wmod_rest_loaded = sem("wmod_rest_loaded")
        wqk_loaded = sem("wqk_loaded")
        wqk_rest_loaded = sem("wqk_rest_loaded")
        wv_loaded = [sem(f"wv_loaded{k}") for k in range(CHUNKS)]
        wo_loaded = [sem(f"wo_loaded{k}") for k in range(CHUNKS)]
        x_loaded = sem("x_loaded")
        xres_loaded = sem("xres_loaded")
        consts = sem("consts")
        c_act = sem("c_act")
        pick_ready = sem("pick_ready")
        mod_psum = sem("mod_psum")
        mod_ready = sem("mod_ready")
        g8 = sem("g8")
        g8_hi = sem("g8_hi")
        g8_ready = sem("g8_ready")
        gate_psum = sem("gate_psum")
        gate_copied = sem("gate_copied")
        wv_hi = sem("wv_hi")
        wv_split = sem("wv_split")
        wo_hi = sem("wo_hi")
        wo_split = sem("wo_split")
        ln_chain = sem("ln_chain")
        ln_var = sem("ln_var")
        ln_rstd = sem("ln_rstd")
        ln_ready = sem("ln_ready")
        ln_psum = sem("ln_psum")
        ht32_ready = sem("ht32_ready")
        ht_hi = sem("ht_hi")
        ht_split = sem("ht_split")
        w_hi = sem("w_hi")
        w_staged = sem("w_staged")
        qk_psum = sem("qk_psum")
        qk_hi = sem("qk_hi")
        qk_split = sem("qk_split")
        v_psum = sem("v_psum")
        v_hi = sem("v_hi")
        v_split = sem("v_split")
        s_psum = sem("s_psum")
        s_masked = sem("s_masked")
        p_exp = sem("p_exp")
        sum_inv = sem("sum_inv")
        p_norm = sem("p_norm")
        p_norm_last = sem("p_norm_last")
        t_psum = sem("t_psum")
        t_hi = sem("t_hi")
        t_split = sem("t_split")
        z_psum = sem("z_psum")
        z_hi = sem("z_hi")
        z_split = sem("z_split")
        o_done = sem("o_done")
        acc_zero = sem("acc_zero")
        acc_gated = sem("acc_gated")
        y_free = sem("y_free")
        x1_ready = sem("x1_ready")

        wv_flat = [w[:].rearrange("p a c n -> p (a c n)") for w in wv]
        wo_flat = [w[:].rearrange("p a n -> p (a n)") for w in wo]
        pick = wo_flat[0][0:B, (CHUNKS - 1) * CHUNK:(CHUNKS - 1) * CHUNK + B * P].rearrange("b (n p) -> b n p", n=B)
        acc = psum[:, ACC_BANK:ACC_BANK + 2, :].rearrange("p k (t n) -> p (k t) n", t=2)

        def walk(eng, step, batch_begin, last_begin, tail):
            step(0, 0, 0, 0, first=True)
            with eng.Fori(0, B - 1) as b:
                batch_begin(b)
                with eng.Fori(0, PAIRS - 1) as p:
                    step(b * H + p * 2 + 1, p * 2 + 1, 1, b)
                    step(b * H + p * 2 + 2, p * 2 + 2, 0, b, pair=p + 1)
                step(b * H + H - 1, H - 1, 1, b, turn=True)
                step(b * H + H, 0, 0, b + 1, new=True)
            last_begin()
            with eng.Fori(0, PAIRS - 1) as p:
                step(p * 2 + (B - 1) * H + 1, p * 2 + 1, 1, B - 1)
                step(p * 2 + (B - 1) * H + 2, p * 2 + 2, 0, B - 1, pair=p + 1)
            step(HEADS - 1, H - 1, 1, B - 1, last=True)
            tail()

        block = ctx.enter_context(nc.Block())

        @block.sync
        def _(sp):
            sp.dma_start(act_c[:], c_d).then_inc(c_loaded, DMA_INC)
            sp.dma_start(xin[:], rows(x, 0)).then_inc(x_loaded, DMA_INC)
            sp.dma_start(wmod[:, :, 0:2 * D], wmod_v[:, :, 0:2 * D]).then_inc(wmod_loaded, DMA_INC)
            sp.dma_start(wqk[:, 0:2, :], wqk_d[:, 0:2, :]).then_inc(wqk_loaded, DMA_INC)
            sp.dma_start(stage[:, 0:CHUNK], wv_d[:, 0:CHUNK]).then_inc(wv_loaded[0], DMA_INC)
            sp.dma_start(wmod[:, :, 2 * D:], wmod_v[:, :, 2 * D:]).then_inc(wmod_rest_loaded, DMA_INC)
            for k in range(1, CHUNKS):
                sp.dma_start(stage[:, k * CHUNK:(k + 1) * CHUNK], wv_d[:, k * CHUNK:(k + 1) * CHUNK])\
                  .then_inc(wv_loaded[k], DMA_INC)
            sp.dma_start(wqk[:, 2:H, :], wqk_d[:, 2:H, :]).then_inc(wqk_rest_loaded, DMA_INC)
            sp.dma_start(wqk[:, H, :], wqk_d[:, 0, :]).then_inc(wqk_rest_loaded, DMA_INC)
            sp.wait_ge(ln_psum, DC)
            sp.dma_start(xin[:], rows(x, 1)).then_inc(x_loaded, DMA_INC)
            sp.dma_start(xres[:], rows(x, 0)).then_inc(xres_loaded, DMA_INC)
            for k in range(CHUNKS):
                sp.wait_ge(wv_split, k + 1)
                sp.dma_start(stage[:, k * CHUNK:(k + 1) * CHUNK], wo_d[:, k * CHUNK:(k + 1) * CHUNK])\
                  .then_inc(wo_loaded[k], DMA_INC)
            sp.wait_ge(wo_split, CHUNKS)
            sp.dma_start(stage[:, 0:up_d.shape[1]], up_d).then_inc(up_loaded, DMA_INC)
            with sp.Fori(0, B - 2) as b:
                sp.wait_ge(ln_psum, b * DC + 2 * DC)
                sp.dma_start(xin[:], rows(x, b + 2)).then_inc(x_loaded, DMA_INC)
                sp.wait_ge(x1_ready, b + 1)
                sp.dma_start(rows(x1, b), y[:]).then_inc(y_free, DMA_INC)
                sp.dma_start(xres[:], rows(x, b + 1)).then_inc(xres_loaded, DMA_INC)
            sp.wait_ge(ln_psum, B * DC)
            sp.wait_ge(y_free, 2 * DMA_INC)
            sp.dma_start(xin[:], rows(x1, 0)).then_inc(x_loaded, DMA_INC)
            sp.wait_ge(x1_ready, B - 1)
            sp.dma_start(rows(x1, B - 2), y[:]).then_inc(y_free, DMA_INC)
            sp.dma_start(xres[:], rows(x, B - 1)).then_inc(xres_loaded, DMA_INC)
            sp.wait_ge(x1_ready, B)
            sp.dma_start(rows(x1, B - 1), y[:]).then_inc(y_free, DMA_INC)
            sp.wait_ge(y_free, DMA_INC * B + DMA_INC)

        @block.gpsimd
        def _(pool):
            pool.memset(ident[:], 0.0).then_inc(consts, 1)
            pool.memset(mask[:], 0.0).then_inc(consts, 1)
            pool.wait_ge(consts, 2)
            pool.affine_select(out=ident[:], in_=ident[:], compare_op=ALU.not_equal, fill=1.0, base=0,
                               pattern=[[-1, P]], channel_multiplier=1).then_inc(consts, 1)
            pool.affine_select(out=mask[:, SEQ - P:], in_=mask[:, SEQ - P:], compare_op=ALU.is_ge, fill=MASKED,
                               base=0, pattern=[[-1, P]], channel_multiplier=1).then_inc(consts, 1)
            pool.memset(minus_half[:], -0.5).then_inc(consts, 1)
            pool.wait_ge(consts, 5)

            def layer_norm_rstd(b):
                pool.wait_ge(ln_var, b + 1)
                pool.tensor_tensor(rstd[:], mv[:, :, 1], minus_half[:], ALU.pow).then_inc(ln_rstd, 1)

            def stage_weights(i, h):
                if not (isinstance(i, int) and i == 0):
                    alone(pool, qk_psum, i * 2)
                src = wqk[:, h, :].rearrange("p (a c e) -> p a c e", a=2, c=DC)
                pool.tensor_copy(ws[0][:], src).then_inc(w_hi, 1)
                alone(pool, w_hi, i + 1)
                pool.tensor_tensor(ws[1][:], src, ws[0][:], ALU.subtract).then_inc(w_staged, 1)

            layer_norm_rstd(0)
            pool.wait_ge(wqk_loaded, DMA_INC)
            stage_weights(0, 0)
            stage_weights(1, 1)

            def step(i, h, odd, b, pair=0, first=False, turn=False, new=False, last=False):
                alone(pool, sum_inv, i * 2 + 1)
                for t in S_ORDER[:-1]:
                    row = probs[:, odd, tile_at(t):tile_at(t + 1)]
                    pool.tensor_scalar(row, row, inv_sum[:, odd, t:t + 1], 1.0, ALU.mult, ALU.mult).then_inc(p_norm, 1)
                if new:
                    add_residual(b - 1)
                if first:
                    layer_norm_rstd(1)
                if first:
                    for k in range(CHUNKS - 1):
                        pool.wait_ge(wo_hi, k + 1)
                        at = slice(k * CHUNK, (k + 1) * CHUNK)
                        pool.tensor_tensor(wo_flat[1][:, at], stage[:, at], wo_flat[0][:, at],
                                           ALU.subtract).then_inc(wo_split, 1)
                if first:
                    pool.wait_ge(wqk_rest_loaded, 2 * DMA_INC)
                if not last:
                    stage_weights(i + 2, 1 if turn else h + 2)
                if turn:
                    layer_norm_rstd(b + 2)

            def add_residual(b):
                pool.wait_ge(acc_gated, b + 2)
                pool.wait_ge(xres_loaded, b * DMA_INC + DMA_INC)
                pool.tensor_tensor(y[:], y[:], xres[:], ALU.add).then_inc(x1_ready, 1)

            walk(pool, step, lambda b: None, lambda: None, lambda: add_residual(B - 1))

        @block.scalar
        def _(act):
            act.wait_ge(c_loaded, DMA_INC)
            act.activation(act_c[:], act_c[:], ACT.Silu).then_inc(c_act, 1)
            act.wait_ge(consts, 3)
            act.activation(pick, ident[0:B, 0:B].rearrange("b (n p) -> b n p", p=1).to_broadcast([B, B, P]),
                           ACT.Copy).then_inc(pick_ready, 1)

            def ht_evacuate(b):
                for c in range(DC):
                    act.wait_ge(ln_psum, b * DC + c + 1)
                    act.activation(ht32[:, c, :], psum[:, ACC_BANK + c, :], ACT.Identity,
                                   bias=mod_t[:, c, bass.ds(b, 1)],
                                   scale=mod_t[:, DC + c, bass.ds(b, 1)]).then_inc(ht32_ready, 1)

            def ht_split_hi(b):
                act.wait_ge(ht32_ready, b * DC + DC)
                act.activation(ht[0][:], ht32[:], ACT.Copy).then_inc(ht_hi, 1)

            def qk_evacuate(i, odd):
                for n, dst in enumerate((qt, kt)):
                    act.wait_ge(qk_psum, i * 2 + n + 1)
                    act.activation(dst[0][:], psum[:, QK_BANK[1 - odd][n], :], ACT.Copy,
                                   scale=(-SCALE, 1.0)[n]).then_inc(qk_hi, 1)

            act.wait_ge(consts, 5)
            act.wait_ge(mod_ready, 1)
            ht_evacuate(0)
            ht_split_hi(0)
            qk_evacuate(0, 0)

            def weights_hi(k, loaded, dst, done):
                act.wait_ge(loaded[k], DMA_INC)
                act.activation(dst[:, k * CHUNK:(k + 1) * CHUNK], stage[:, k * CHUNK:(k + 1) * CHUNK],
                               ACT.Copy).then_inc(done, 1)

            weights_hi(0, wv_loaded, wv_flat[0], wv_hi)

            def step(i, h, odd, b, pair=0, first=False, turn=False, new=False, last=False):
                if turn:
                    act.wait_ge(v_psum, b * H + H)
                    act.wait_ge(qk_psum, b * 2 * H + 2 * H)
                    ht_split_hi(b + 1)
                for n, t in enumerate(S_ORDER):
                    act.wait_ge(s_masked, i * NT + n + 1)
                    row = probs[:, odd, tile_at(t):tile_at(t + 1)]
                    act.activation(row, row, ACT.Exp, bias=neg_max[:, odd, t:t + 1], scale=-1.0,
                                   accum_out=row_sum[:, odd, t:t + 1]).then_inc(p_exp, 1)
                if not first:
                    z_evacuate(i - 1, 1 - odd)
                if not last:
                    qk_evacuate(i + 1, 1 - odd)
                if not odd:
                    for half in range(2):
                        act.wait_ge(v_psum, i + half + 1)
                        act.activation(v[0][:, 2 * half:2 * half + 2, :].rearrange("p t n -> p (t n)"),
                                       psum[:, V_BANK[half], :], ACT.Copy).then_inc(v_hi, 1)
                for n in range(3):
                    act.wait_ge(t_psum, i * 3 + n + 1)
                    act.activation(pt[0][:, n * 4 * P:n * 4 * P + T_WIDTH[n]],
                                   psum[:, T_BANK[odd][n], 0:T_WIDTH[n]], ACT.Copy).then_inc(t_hi, 1)
                if first:
                    for k in range(1, CHUNKS):
                        weights_hi(k, wv_loaded, wv_flat[0], wv_hi)
                        if k == 1:
                            act.wait_ge(g8, 5)
                            act.activation(gates8_parts[0], gates8[:], ACT.Copy).then_inc(g8_hi, 1)
                    for k in range(CHUNKS):
                        if k < CHUNKS - 1:
                            weights_hi(k, wo_loaded, wo_flat[0], wo_hi)
                        for n in (2 * k, 2 * k + 1):
                            act.wait_ge(gate_psum, n + 1)
                            act.activation(gates[:, n, :], psum[:, ACC_BANK + n % 2, :], ACT.Copy)\
                               .then_inc(gate_copied, 1)
                    weights_hi(CHUNKS - 1, wo_loaded, wo_flat[0], wo_hi)

            def z_evacuate(i, odd):
                act.wait_ge(z_psum, i + 1)
                act.activation(z[0][:], psum[:, Z_BANK[1 - odd], :], ACT.Copy).then_inc(z_hi, 1)

            def zero_acc(k):
                act.activation(psum[:, ACC_BANK + k, :], mask[:, 0:1].to_broadcast([P, SEQ]), ACT.Copy).then_inc(acc_zero, 1)

            def batch_begin(b):
                ht_evacuate(b + 1)
                for k in range(2):
                    act.wait_ge(ht32_ready, (b + 1) * DC + k + 1)
                    zero_acc(k)

            def last_begin():
                act.wait_ge(acc_gated, B)
                for k in range(2):
                    zero_acc(k)

            walk(act, step, batch_begin, last_begin, lambda: z_evacuate(HEADS - 1, 1))

        @block.vector
        def _(dve):
            def layer_norm_statistics(b):
                dve.wait_ge(x_loaded, b * DMA_INC + DMA_INC)
                for t in range(NT):
                    dve.bn_stats(stats[:, t, :], xin[:, t, :]).then_inc(ln_chain, 1)
                alone(dve, ln_chain, b * 2 * NT + NT)
                for t in range(NT):
                    dve.bn_aggr(mv[:, t, :], stats[:, t, :]).then_inc(ln_chain, 1)
                dve.wait_ge(ln_chain, b * 2 * NT + 2 * NT)
                dve.tensor_scalar(mv[:, :, 1], mv[:, :, 1], LN_EPS, None, ALU.add).then_inc(ln_var, 1)

            def layer_norm_apply(b):
                dve.wait_ge(ln_rstd, b + 1)
                for t in range(NT):
                    last = dve.tensor_scalar(xin[:, t, :], xin[:, t, :], mv[:, t, 0:1], rstd[:, t:t + 1],
                                             ALU.subtract, ALU.mult)
                last.then_inc(ln_ready, 1)

            def ht_split_lo(b):
                dve.wait_ge(ht_hi, b + 1)
                dve.tensor_tensor(ht[1][:], ht32[:], ht[0][:], ALU.subtract).then_inc(ht_split, 1)

            def qk_lo(i, odd):
                for n, dst in enumerate((qt, kt)):
                    dve.wait_ge(qk_hi, i * 2 + n + 1)
                    dve.scalar_tensor_tensor(out=dst[1][:], in0=psum[:, QK_BANK[1 - odd][n], :],
                                             scalar=(-SCALE, 1.0)[n], in1=dst[0][:], op0=ALU.mult,
                                             op1=ALU.subtract).then_inc(qk_split, 1)

            dve.sem_inc(y_free, DMA_INC)
            dve.sem_inc(acc_gated, 1)
            layer_norm_statistics(0)
            layer_norm_apply(0)

            def shift_and_scale(k, bank):
                src = psum[:, bank, 0:2 * DC * B].rearrange("p (k b) -> p k b", b=B)
                at = 2 * k * DC
                dve.tensor_copy(mod_t[:, at:at + DC, :], src[:, 0:DC, :])
                return dve.tensor_scalar(mod_t[:, at + DC:at + 2 * DC, :], src[:, DC:, :], 1.0, None, ALU.add)

            dve.wait_ge(mod_psum, 1)
            shift_and_scale(0, 0).then_inc(mod_ready, 1)
            ht_split_lo(0)
            qk_lo(0, 0)

            def weights_lo(k, hi, parts, split):
                dve.wait_ge(hi, k + 1)
                at = slice(k * CHUNK, (k + 1) * CHUNK)
                dve.tensor_tensor(parts[1][:, at], stage[:, at], parts[0][:, at], ALU.subtract).then_inc(split, 1)

            weights_lo(0, wv_hi, wv_flat, wv_split)

            def second_modulation():
                dve.wait_ge(mod_psum, 2)
                shift_and_scale(1, ACC_BANK).then_inc(mod_ready, 1)
                dve.wait_ge(mod_psum, 3)
                dve.tensor_copy(gates8[:], psum[0:B, ACC_BANK + 1, :]).then_inc(g8, 1)
                dve.wait_ge(g8, 1)
                dve.tensor_scalar(gates8s, gates8[:], 0.0, 2.0, ALU.is_ge, ALU.mult).then_inc(g8, 1)
                dve.scalar_tensor_tensor(out=gates8a, in0=gates8[:], scalar=-1.0, in1=gates8[:],
                                         op0=ALU.mult, op1=ALU.max).then_inc(g8, 1)
                dve.wait_ge(g8, 3)
                dve.tensor_scalar(gates8a, gates8a, GATE_MIN, None, ALU.max).then_inc(g8, 1)
                dve.wait_ge(g8, 4)
                dve.scalar_tensor_tensor(out=gates8[:], in0=gates8s, scalar=-1.0, in1=gates8a,
                                         op0=ALU.add, op1=ALU.mult).then_inc(g8, 1)

            def weights_and_gates():
                for k in range(1, CHUNKS):
                    weights_lo(k, wv_hi, wv_flat, wv_split)
                    if k == 1:
                        dve.wait_ge(g8_hi, 1)
                        dve.tensor_tensor(gates8_parts[1], gates8[:], gates8_parts[0], ALU.subtract).then_inc(g8_ready, 1)
                layer_norm_statistics(1)
                layer_norm_apply(1)
                dve.wait_ge(wo_split, CHUNKS - 1)
                weights_lo(CHUNKS - 1, wo_hi, wo_flat, wo_split)

            def z_lo(i, odd):
                dve.wait_ge(z_hi, i + 1)
                dve.tensor_tensor(z[1][:], psum[:, Z_BANK[1 - odd], :], z[0][:], ALU.subtract).then_inc(z_split, 1)

            def gate_output(b):
                dve.wait_ge(o_done, b * H + H)
                dve.wait_ge(y_free, b * DMA_INC + DMA_INC)
                for k in range(2):
                    last = dve.tensor_tensor(
                        y[:, 2 * k:2 * k + 2, :], acc[:, 2 * k:2 * k + 2, :],
                        gates[:, bass.ds(b, 1), 0:D].to_broadcast([P, 2, D]), ALU.mult)
                last.then_inc(acc_gated, 1)

            def step(i, h, odd, b, pair=0, first=False, turn=False, new=False, last=False):
                if turn:
                    ht_split_lo(b + 1)
                for n, t in enumerate(S_ORDER):
                    alone(dve, s_psum, i * 3 + (1, 2, 2, 3)[n])
                    width = P * (t + 1)
                    dve.tensor_tensor_reduce(
                        out=probs[:, odd, tile_at(t):tile_at(t + 1)],
                        in0=psum[:, S_BANK[odd][t], S_COL[t]:S_COL[t] + width], in1=mask[:, SEQ - width:],
                        scale=1.0, scalar=HUGE, op0=ALU.add, op1=ALU.min,
                        accum_out=neg_max[:, odd, t:t + 1]).then_inc(s_masked, 1)
                if not first:
                    z_lo(i - 1, 1 - odd)
                dve.wait_ge(p_exp, i * NT + NT - 1)
                dve.reciprocal(inv_sum[:, odd, 0:NT - 1], row_sum[:, odd, 0:NT - 1]).then_inc(sum_inv, 1)
                dve.wait_ge(p_exp, i * NT + NT)
                dve.reciprocal(inv_sum[:, odd, NT - 1:], row_sum[:, odd, NT - 1:]).then_inc(sum_inv, 1)
                dve.wait_ge(sum_inv, i * 2 + 2)
                row = probs[:, odd, tile_at(NT - 1):]
                dve.tensor_scalar(row, row, inv_sum[:, odd, NT - 1:], None, ALU.mult).then_inc(p_norm_last, 1)
                if not last:
                    qk_lo(i + 1, 1 - odd)
                if turn:
                    layer_norm_statistics(b + 2)
                if new:
                    gate_output(b - 1)
                    layer_norm_apply(b + 1)
                if first:
                    second_modulation()
                if not odd:
                    for half in range(2):
                        dve.wait_ge(v_hi, i + half + 1)
                        out = v[1][:, 2 * half:2 * half + 2, :].rearrange("p t n -> p (t n)")
                        hi = v[0][:, 2 * half:2 * half + 2, :].rearrange("p t n -> p (t n)")
                        dve.tensor_tensor(out, psum[:, V_BANK[half], :], hi, ALU.subtract).then_inc(v_split, 1)
                for n in range(3):
                    dve.wait_ge(t_hi, i * 3 + n + 1)
                    at = slice(n * 4 * P, n * 4 * P + T_WIDTH[n])
                    dve.tensor_tensor(pt[1][:, at], psum[:, T_BANK[odd][n], 0:T_WIDTH[n]], pt[0][:, at],
                                      ALU.subtract).then_inc(t_split, 1)
                if first:
                    weights_and_gates()

            def tail():
                z_lo(HEADS - 1, 1)
                gate_output(B - 1)

            walk(dve, step, lambda b: None, lambda: None, tail)

        @block.tensor
        def _(pe):
            def split_product(out, stationary, moving, start, stop, skip=False):
                for n, (s, m) in enumerate(PASSES):
                    last = pe.matmul(out, stationary(s), moving(m), start=start and n == 0,
                                     stop=stop and n == len(PASSES) - 1, skip_group_check=skip)
                return last

            def layer_norm_transposes(b):
                pe.wait_ge(ln_ready, b + 1)
                for c in range(DC):
                    for t in range(NT):
                        last = pe.transpose(psum[:, ACC_BANK + c, t * P:(t + 1) * P],
                                            xin[:, t, c * P:(c + 1) * P], ident[:])
                    last.then_inc(ln_psum, 1)

            def queries_keys(i, odd):
                pe.wait_ge(w_staged, i + 1)
                for n in range(2):
                    for c in range(DC):
                        last = split_product(psum[:, QK_BANK[1 - odd][n], :], lambda s: ws[s][:, n, c, :],
                                             lambda m: ht[m][:, c, :], c == 0, c == DC - 1)
                    last.then_inc(qk_psum, 1)

            def modulation(first_cols, bank):
                at = 0
                for first_col in first_cols:
                    for col in range(first_col, first_col + D, P):
                        for c in range(DC):
                            last = pe.matmul(psum[:, bank, at:at + B], wmod[:, c, col:col + P], act_c[:, c, :],
                                             start=(c == 0), stop=(c == DC - 1))
                        at += B
                last.then_inc(mod_psum, 1)

            pe.wait_ge(c_act, 1)
            pe.wait_ge(wmod_loaded, DMA_INC)
            modulation((0, D), 0)
            pe.wait_ge(consts, 5)
            layer_norm_transposes(0)
            pe.wait_ge(ht_split, 1)
            queries_keys(0, 0)
            pe.wait_ge(wmod_rest_loaded, DMA_INC)
            modulation((3 * D, 4 * D), ACC_BANK)
            for k in range(2):
                for c in range(DC):
                    last = pe.matmul(psum[0:B, ACC_BANK + 1, k * D:(k + 1) * D], act_c[:, c, :],
                                     wmod[:, c, (3 * k + 2) * D:(3 * k + 3) * D],
                                     start=(c == 0), stop=(c == DC - 1))
            last.then_inc(mod_psum, 1)

            def gates_to_all():
                pe.wait_ge(pick_ready, 1)
                pe.wait_ge(g8_ready, 1)
                for b in range(B):
                    if b >= 2:
                        pe.wait_ge(gate_copied, b - 1)
                    for n, part in enumerate(gates8_parts):
                        last = pe.matmul(psum[:, ACC_BANK + b % 2, :], pick[:, b, :], part,
                                         start=(n == 0), stop=(n == 1))
                    last.then_inc(gate_psum, 1)
                pe.wait_ge(gate_copied, B)

            def scores(i, odd):
                pe.wait_ge(qk_split, i * 2 + 2)
                for n, t in enumerate(S_ORDER):
                    if t == 3:
                        if odd:
                            pe.wait_ge(v_split, i + 1)
                    width = P * (t + 1)
                    last = split_product(psum[:, S_BANK[odd][t], S_COL[t]:S_COL[t] + width],
                                         lambda s: qt[s][:, t * P:(t + 1) * P], lambda m: kt[m][:, 0:width],
                                         True, True)
                    if t != 0:
                        last.then_inc(s_psum, 1)

            def weighted_values(i, odd):
                for n, j in enumerate(J_ORDER):
                    if n != 2:
                        pe.wait_ge(t_split, i * 3 + (1, 2, 0, 3)[n])
                    width = SEQ - P * j
                    last = split_product(psum[:, Z_BANK[1 - odd], P * j:], lambda s: v[s][:, j, odd * P:(odd + 1) * P],
                                         lambda m: pt[m][:, PT_AT[j]:PT_AT[j] + width], n == 0, n == NT - 1)
                last.then_inc(z_psum, 1)

            def project(i, h):
                pe.wait_ge(z_split, i + 1)
                for t in range(NT):
                    last = split_product(acc[:, t, :], lambda s: z[s][:, t * P:(t + 1) * P],
                                         lambda m: wo[m][:, h, :], False, True, skip=True)
                last.then_inc(o_done, 1)

            def values(i, pair):
                pe.wait_ge(s_masked, i * NT + 1)
                for t in range(NT):
                    for c in range(DC):
                        last = split_product(psum[:, V_BANK[t // 2], (t % 2) * 2 * P:(t % 2 + 1) * 2 * P],
                                             lambda s: ht[s][:, c, t * P:(t + 1) * P],
                                             lambda m: wv[m][:, pair, c, :], c == 0, c == DC - 1)
                    if t % 2:
                        last.then_inc(v_psum, 1)

            def transposes(i, odd):
                pe.wait_ge(p_norm, i * (NT - 1) + NT - 1)
                for tiles in (range(NT - 1), range(NT - 1, NT)):
                    if NT - 1 in tiles:
                        pe.wait_ge(p_norm_last, i + 1)
                    for n, held in enumerate(T_HOLDS):
                        if not odd and n == 2 and NT - 1 not in tiles:
                            pe.wait_ge(v_split, i + 1)
                        for j, col in held:
                            for t in tiles:
                                if t >= j:
                                    last = pe.transpose(
                                        psum[:, T_BANK[odd][n], col + (t - j) * P:col + (t - j + 1) * P],
                                        probs[:, odd, tile_at(t) + j * P:tile_at(t) + (j + 1) * P], ident[:])
                        if NT - 1 in tiles:
                            last.then_inc(t_psum, 1)

            def step(i, h, odd, b, pair=0, first=False, turn=False, new=False, last=False):
                scores(i, odd)
                if not first:
                    weighted_values(i - 1, 1 - odd)
                if turn:
                    pe.wait_ge(ht_split, b + 2)
                if not last:
                    queries_keys(i + 1, 1 - odd)
                if not first:
                    if not new:
                        pe.wait_ge(acc_zero, b * 2 + 2)
                    project(i - 1, H - 1 if new else h - 1)
                if not odd:
                    if first:
                        pe.wait_ge(wv_split, 1)
                    values(i, pair)
                transposes(i, odd)
                if first:
                    gates_to_all()

            def batch_begin(b):
                pe.wait_ge(acc_gated, b + 1)
                layer_norm_transposes(b + 1)
                pe.wait_ge(wo_split, CHUNKS)

            def tail():
                weighted_values(HEADS - 1, 1)
                project(HEADS - 1, H - 1)

            walk(pe, step, batch_begin, lambda: None, tail)


def feed_forward_layer(nc, psum, stage, mod_t, gates, ident, x1, up_loaded, down_d, wg_d, bg_d, bgate_d, bup_d,
                       bsup_d, bdown_d, bsdown_d, out):
    B, SEQ, D = x1.shape
    NT = SEQ // P
    DC = D // P
    NE = bgate_d.shape[1]
    NS = bsup_d.shape[1]
    NG = wg_d.shape[2]
    KEPT = NE
    UPS = NS + 2 * NE
    UP, HID, DOWN = NS + 2 * NE, NS + NE, NE + 1
    ROUTE = 9
    Y_BANK = (4, 6)
    LOGIT_T_BANK, LOGIT_BANK, WEIGHT_T_BANK = 2, 3, 6

    with ExitStack() as ctx:
        def sb(name, shape, dt=F32):
            return ctx.enter_context(nc.sbuf_tensor(name, shape, dt))

        def sem(name):
            return ctx.enter_context(nc.semaphore(name))

        def pair_of(name, shape):
            return [sb(name + "_hi", shape, F32R), sb(name + "_lo", shape, F32R)]

        up = pair_of("f_up", [P, UPS, DC, P])
        down_raw = sb("f_down_raw", [P, NE + NS, D])
        down = pair_of("f_down", [P, NE + NS, D])
        wg = sb("f_wg", [P, DC, NG])
        bg = sb("f_bg", [NG, 1])
        b_gate = sb("f_b_gate", [P, NE])
        b_up = sb("f_b_up", [P, NE])
        b_sup = sb("f_b_sup", [P, NS])
        b_out = sb("f_b_out", [NE + 1, D])
        minus_half = sb("f_minus_half", [P, NT])
        earlier = sb("f_earlier", [P, NG, NG])
        xin = sb("f_xin", [P, NT, D])
        stats = sb("f_stats", [P, NT, 6])
        mv = sb("f_mv", [P, NT, 2])
        rstd = sb("f_rstd", [P, NT])
        ht32 = sb("f_ht32", [P, DC, SEQ])
        ht = pair_of("f_ht", [P, DC, SEQ])
        logit_t = sb("f_logit_t", [NG, SEQ])
        logit = sb("f_logit", [P, NT, NG])
        top = sb("f_top", [P, NT])
        above = sb("f_above", [P, NT, NG, NG])
        equal = sb("f_equal", [P, NT, NG, NG])
        rank = sb("f_rank", [P, NT, NG])
        kept = sb("f_kept", [P, NT, NG])
        shifted = sb("f_shifted", [P, NT, NG])
        weight = sb("f_weight", [P, NT, NG])
        total = sb("f_total", [P, NT])
        inv_total = sb("f_inv_total", [P, NT])
        weight1 = sb("f_weight1", [P, NT, NE + 1])
        weight_t = sb("f_weight_t", [NE + 1, SEQ])
        gated = sb("f_gated", [P, 2, SEQ])
        hid32 = sb("f_hid32", [P, 2, SEQ])
        hid = [pair_of(f"f_hid{n}", [P, SEQ]) for n in range(2)]
        shid32 = sb("f_shid32", [P, NS, SEQ])
        shid = [pair_of(f"f_shid{n}", [P, SEQ]) for n in range(NS)]
        f = sb("f_sum", [P, NT, D])
        xres = sb("f_xres", [P, NT, D])
        y = sb("f_y", [P, NT, D])

        down_loaded = sem("f_down_loaded")
        small_loaded = sem("f_small_loaded")
        x_loaded = sem("f_x_loaded")
        xres_loaded = sem("f_xres_loaded")
        y_free = sem("f_y_free")
        consts = sem("f_consts")
        up_hi = sem("f_up_hi")
        up_split = sem("f_up_split")
        down_hi = sem("f_down_hi")
        down_split = sem("f_down_split")
        ln_chain = sem("f_ln_chain")
        ln_var = sem("f_ln_var")
        ln_rstd = sem("f_ln_rstd")
        ln_ready = sem("f_ln_ready")
        ln_psum = sem("f_ln_psum")
        ht32_ready = sem("f_ht32_ready")
        ht_hi = sem("f_ht_hi")
        ht_split = sem("f_ht_split")
        logit_t_psum = sem("f_logit_t_psum")
        logit_t_ready = sem("f_logit_t_ready")
        logit_psum = sem("f_logit_psum")
        route = sem("f_route")
        shifted_ready = sem("f_shifted_ready")
        weight_exp = sem("f_weight_exp")
        weight_ready = sem("f_weight_ready")
        weight_t_psum = sem("f_weight_t_psum")
        weight_t_ready = sem("f_weight_t_ready")
        up_psum = sem("f_up_psum")
        silu_done = sem("f_silu_done")
        glu_done = sem("f_glu_done")
        hid_hi = sem("f_hid_hi")
        hid_split = sem("f_hid_split")
        down_psum = sem("f_down_psum")
        summed = sem("f_summed")
        f_read = sem("f_f_read")
        y_ready = sem("f_y_ready")

        def y_bank(k):
            return psum[:, Y_BANK[k]:Y_BANK[k] + 2, :].rearrange("p k (t n) -> p (k t) n", t=2)

        block = ctx.enter_context(nc.Block())

        @block.sync
        def _(sp):
            sp.dma_start(xin[:], rows(x1, 0)).then_inc(x_loaded, DMA_INC)
            sp.dma_start(down_raw[:].rearrange("p a n -> p (a n)"), down_d).then_inc(down_loaded, DMA_INC)
            for dst, src in ((wg, wg_d), (bg, bg_d), (b_gate, bgate_d), (b_up, bup_d), (b_sup, bsup_d)):
                sp.dma_start(dst[:], src).then_inc(small_loaded, DMA_INC)
            sp.dma_start(b_out[0:NE, :], bdown_d).then_inc(small_loaded, DMA_INC)
            sp.dma_start(b_out[NE:NE + 1, :], bsdown_d).then_inc(small_loaded, DMA_INC)
            with sp.Fori(0, B - 1) as b:
                sp.wait_ge(ln_psum, b * DC + DC)
                sp.dma_start(xin[:], rows(x1, b + 1)).then_inc(x_loaded, DMA_INC)
                sp.dma_start(xres[:], rows(x1, b)).then_inc(xres_loaded, DMA_INC)
                sp.wait_ge(y_ready, b + 1)
                sp.dma_start(rows(out, b), y[:]).then_inc(y_free, DMA_INC)
            sp.dma_start(xres[:], rows(x1, B - 1)).then_inc(xres_loaded, DMA_INC)
            sp.wait_ge(y_ready, B)
            sp.dma_start(rows(out, B - 1), y[:]).then_inc(y_free, DMA_INC)
            sp.wait_ge(y_free, B * DMA_INC + DMA_INC)

        @block.gpsimd
        def _(pool):
            pool.memset(minus_half[:], -0.5).then_inc(consts, 1)
            pool.memset(earlier[:], 1.0).then_inc(consts, 1)
            pool.memset(weight1[:], 1.0).then_inc(consts, 1)
            pool.wait_ge(consts, 3)
            pool.affine_select(out=earlier[:], in_=earlier[:], compare_op=ALU.is_ge, fill=0.0, base=-1,
                               pattern=[[1, NG], [-1, NG]], channel_multiplier=0).then_inc(consts, 1)

            def layer_norm_rstd(b):
                pool.wait_ge(ln_var, b + 1)
                pool.tensor_tensor(rstd[:], mv[:, :, 1], minus_half[:], ALU.pow).then_inc(ln_rstd, 1)

            def finish(b):
                pool.wait_ge(summed, b * DOWN + DOWN + 1)
                alone(pool, y_free, b * DMA_INC + DMA_INC)
                gate = gates[:, bass.ds(b, 1), D:2 * D].to_broadcast([P, NT, D])
                pool.tensor_tensor(y[:], f[:], gate, ALU.mult).then_inc(f_read, 1)
                pool.wait_ge(xres_loaded, b * DMA_INC + DMA_INC)
                alone(pool, f_read, b + 2)
                pool.tensor_tensor(y[:], y[:], xres[:], ALU.add).then_inc(y_ready, 1)

            layer_norm_rstd(0)
            with pool.Fori(0, B - 1) as b:
                layer_norm_rstd(b + 1)
                finish(b)
            finish(B - 1)

        @block.scalar
        def _(act):
            def ht_evacuate(b):
                for c in range(DC):
                    act.wait_ge(ln_psum, b * DC + c + 1)
                    act.activation(ht32[:, c, :], psum[:, Y_BANK[0] + c, :], ACT.Identity,
                                   bias=mod_t[:, 2 * DC + c, bass.ds(b, 1)],
                                   scale=mod_t[:, 3 * DC + c, bass.ds(b, 1)]).then_inc(ht32_ready, 1)

            def ht_split_hi(b):
                act.wait_ge(ht32_ready, b * DC + DC)
                act.activation(ht[0][:], ht32[:], ACT.Copy).then_inc(ht_hi, 1)

            act.wait_ge(up_loaded, DMA_INC)
            act.activation(up[0][:].rearrange("p a c n -> p (a c n)"), stage[:, 0:UPS * DC * P],
                           ACT.Copy).then_inc(up_hi, 1)
            ht_evacuate(0)
            ht_split_hi(0)
            act.wait_ge(down_loaded, DMA_INC)
            act.activation(down[0][:], down_raw[:], ACT.Copy).then_inc(down_hi, 1)
            act.wait_ge(small_loaded, 7 * DMA_INC)

            def hi(b, n, dst, src):
                act.activation(dst[0][:], src, ACT.Copy).then_inc(hid_hi, 1)

            def batch(b, last=False):
                act.wait_ge(logit_t_psum, b + 1)
                act.activation(logit_t[:], psum[0:NG, LOGIT_T_BANK, :], ACT.Identity,
                               bias=bg[:]).then_inc(logit_t_ready, 1)
                for m in range(NS):
                    act.wait_ge(up_psum, b * UP + m + 1)
                    act.activation(shid32[:, m, :], psum[:, m, :], ACT.Silu,
                                   bias=b_sup[:, m:m + 1]).then_inc(silu_done, 1)
                    act.wait_ge(silu_done, b * HID + m + 1)
                    hi(b, m, shid[m], shid32[:, m, :])
                for n in range(NE):
                    act.wait_ge(up_psum, b * UP + NS + 2 * n + 1)
                    act.activation(gated[:, n % 2, :], psum[:, n % 2, :], ACT.Silu,
                                   bias=b_gate[:, n:n + 1]).then_inc(silu_done, 1)
                    act.wait_ge(glu_done, b * NE + n + 1)
                    hi(b, NS + n, hid[n % 2], hid32[:, n % 2, :])
                    if n == 0:
                        act.wait_ge(shifted_ready, b + 1)
                        act.activation(weight[:], shifted[:], ACT.Exp).then_inc(weight_exp, 1)
                    if n == 1:
                        act.wait_ge(weight_t_psum, b + 1)
                        act.activation(weight_t[:], psum[0:NE + 1, WEIGHT_T_BANK, :], ACT.Copy).then_inc(weight_t_ready, 1)
                    if n == NE - 2 and not last:
                        ht_evacuate(b + 1)
                if not last:
                    act.wait_ge(up_psum, b * UP + UP)
                    ht_split_hi(b + 1)

            with act.Fori(0, B - 1) as b:
                batch(b)
            batch(B - 1, last=True)

        @block.vector
        def _(dve):
            def layer_norm(b):
                dve.wait_ge(x_loaded, b * DMA_INC + DMA_INC)
                for t in range(NT):
                    dve.bn_stats(stats[:, t, :], xin[:, t, :]).then_inc(ln_chain, 1)
                alone(dve, ln_chain, b * 2 * NT + NT)
                for t in range(NT):
                    dve.bn_aggr(mv[:, t, :], stats[:, t, :]).then_inc(ln_chain, 1)
                dve.wait_ge(ln_chain, b * 2 * NT + 2 * NT)
                dve.tensor_scalar(mv[:, :, 1], mv[:, :, 1], LN_EPS, None, ALU.add).then_inc(ln_var, 1)
                dve.wait_ge(ln_rstd, b + 1)
                for t in range(NT):
                    last = dve.tensor_scalar(xin[:, t, :], xin[:, t, :], mv[:, t, 0:1], rstd[:, t:t + 1],
                                             ALU.subtract, ALU.mult)
                last.then_inc(ln_ready, 1)

            def ht_split_lo(b):
                dve.wait_ge(ht_hi, b + 1)
                dve.tensor_tensor(ht[1][:], ht32[:], ht[0][:], ALU.subtract).then_inc(ht_split, 1)

            dve.sem_inc(y_free, DMA_INC)
            dve.sem_inc(summed, 1)
            dve.sem_inc(f_read, 1)
            layer_norm(0)
            dve.wait_ge(up_hi, 1)
            dve.tensor_tensor(up[1][:].rearrange("p a c n -> p (a c n)"), stage[:, 0:UPS * DC * P],
                              up[0][:].rearrange("p a c n -> p (a c n)"), ALU.subtract).then_inc(up_split, 1)
            ht_split_lo(0)
            dve.wait_ge(down_hi, 1)
            dve.tensor_tensor(down[1][:], down_raw[:], down[0][:], ALU.subtract).then_inc(down_split, 1)
            dve.wait_ge(consts, 4)

            def lo(b, n, dst, src):
                dve.wait_ge(hid_hi, b * HID + n + 1)
                dve.tensor_tensor(dst[1][:], src, dst[0][:], ALU.subtract).then_inc(hid_split, 1)

            def ranks(b):
                dve.wait_ge(logit_psum, b + 1)
                dve.tensor_copy(logit[:].rearrange("p t n -> p (t n)"), psum[:, LOGIT_BANK, 0:NT * NG]).then_inc(route, 1)
                dve.wait_ge(route, b * ROUTE + 1)
                by_j = logit[:].rearrange("p t (i n) -> p t i n", i=1).to_broadcast([P, NT, NG, NG])
                by_i = logit[:].rearrange("p t (n i) -> p t n i", i=1).to_broadcast([P, NT, NG, NG])
                dve.tensor_tensor(above[:], by_j, by_i, ALU.is_gt).then_inc(route, 1)
                dve.tensor_tensor(equal[:], by_j, by_i, ALU.is_equal).then_inc(route, 1)
                dve.tensor_reduce(top[:], logit[:], AX_X, ALU.max).then_inc(route, 1)
                dve.wait_ge(route, b * ROUTE + 4)
                dve.tensor_tensor(shifted[:], logit[:], top[:].rearrange("p (t i) -> p t i", i=1).to_broadcast([P, NT, NG]),
                                  ALU.subtract).then_inc(shifted_ready, 1)
                for t in range(NT):
                    last = dve.tensor_tensor(equal[:, t, :, :], equal[:, t, :, :], earlier[:], ALU.mult)
                last.then_inc(route, 1)
                dve.wait_ge(route, b * ROUTE + 5)
                dve.tensor_tensor(above[:], above[:], equal[:], ALU.add).then_inc(route, 1)
                dve.wait_ge(route, b * ROUTE + 6)
                dve.tensor_reduce(rank[:], above[:], AX_X, ALU.add).then_inc(route, 1)

            def weights(b):
                dve.wait_ge(route, b * ROUTE + 7)
                dve.wait_ge(weight_exp, b + 1)
                dve.scalar_tensor_tensor(out=kept[:], in0=rank[:], scalar=float(KEPT), in1=weight[:],
                                         op0=ALU.is_lt, op1=ALU.mult).then_inc(route, 1)
                dve.wait_ge(route, b * ROUTE + 8)
                dve.tensor_reduce(total[:], kept[:], AX_X, ALU.add).then_inc(route, 1)
                dve.wait_ge(route, b * ROUTE + 9)
                dve.reciprocal(inv_total[:], total[:]).then_inc(weight_ready, 1)
                dve.wait_ge(weight_ready, b * 2 + 1)
                dve.tensor_tensor(weight1[:, :, 0:NE], kept[:, :, 0:NE],
                                  inv_total[:].rearrange("p (t i) -> p t i", i=1).to_broadcast([P, NT, NE]),
                                  ALU.mult).then_inc(weight_ready, 1)

            def glu(b, n):
                dve.wait_ge(up_psum, b * UP + NS + 2 * n + 2)
                dve.wait_ge(silu_done, b * HID + NS + n + 1)
                dve.scalar_tensor_tensor(out=hid32[:, n % 2, :], in0=psum[:, 2 + n % 2, :], scalar=b_up[:, n:n + 1],
                                         in1=gated[:, n % 2, :], op0=ALU.add, op1=ALU.mult).then_inc(glu_done, 1)

            def add_expert(b, n):
                if n == 0:
                    dve.wait_ge(f_read, b + 1)
                    dve.wait_ge(weight_ready, b * 2 + 2)
                dve.wait_ge(down_psum, b * DOWN + (n + 1 if n < NE - 1 else DOWN))
                src = y_bank(n % 2 if n < NE - 2 else 1)
                for t in range(NT):
                    w = weight1[:, t, n:n + 1]
                    if n == 0:
                        last = dve.tensor_scalar(f[:, t, :], src[:, t, :], w, None, ALU.mult)
                    else:
                        last = dve.scalar_tensor_tensor(out=f[:, t, :], in0=src[:, t, :], scalar=w, in1=f[:, t, :],
                                                        op0=ALU.mult, op1=ALU.add)
                last.then_inc(summed, 1)

            def add_shared(b):
                dve.wait_ge(down_psum, b * DOWN + DOWN - 1)
                for k in range(2):
                    last = dve.tensor_tensor(f[:, 2 * k:2 * k + 2, :], y_bank(0)[:, 2 * k:2 * k + 2, :],
                                             f[:, 2 * k:2 * k + 2, :], ALU.add)
                last.then_inc(summed, 1)

            def batch(b, last=False):
                lo(b, 0, shid[0], shid32[:, 0, :])
                ranks(b)
                lo(b, 1, shid[1], shid32[:, 1, :])
                for n in range(NE):
                    glu(b, n)
                    if n == 2 and not last:
                        layer_norm(b + 1)
                    lo(b, NS + n, hid[n % 2], hid32[:, n % 2, :])
                    if n == 0:
                        weights(b)
                    if n >= 1:
                        dve.wait_ge(summed, b * DOWN + n)
                        add_expert(b, n - 1)
                if not last:
                    ht_split_lo(b + 1)
                dve.wait_ge(summed, b * DOWN + NE)
                add_shared(b)
                dve.wait_ge(summed, b * DOWN + NE + 1)
                add_expert(b, NE - 1)

            with dve.Fori(0, B - 1) as b:
                batch(b)
            batch(B - 1, last=True)

        @block.tensor
        def _(pe):
            def split_product(out, stationary, moving, start, stop):
                for n, (s, m) in enumerate(PASSES):
                    last = pe.matmul(out, stationary(s), moving(m), start=start and n == 0,
                                     stop=stop and n == len(PASSES) - 1)
                return last

            def layer_norm_transposes(b):
                pe.wait_ge(ln_ready, b + 1)
                for c in range(DC):
                    for t in range(NT):
                        last = pe.transpose(psum[:, Y_BANK[0] + c, t * P:(t + 1) * P],
                                            xin[:, t, c * P:(c + 1) * P], ident[:])
                    last.then_inc(ln_psum, 1)

            def up_product(k, bank):
                for c in range(DC):
                    last = split_product(psum[:, bank, :], lambda s: up[s][:, k, c, :], lambda m: ht[m][:, c, :],
                                         c == 0, c == DC - 1)
                last.then_inc(up_psum, 1)

            def down_product(b, n):
                pe.wait_ge(hid_split, b * HID + NS + n + 1)
                dst = y_bank(n % 2 if n < NE - 2 else 1)
                for t in range(NT):
                    last = split_product(dst[:, t, :], lambda s: hid[n % 2][s][:, t * P:(t + 1) * P],
                                         lambda m: down[m][:, n, :], True, True)
                last.then_inc(down_psum, 1)

            def shared_down_product(b):
                pe.wait_ge(hid_split, b * HID + NS)
                pe.wait_ge(weight_t_ready, b + 1)
                for t in range(NT):
                    dst = y_bank(0)[:, t, :]
                    for m in range(NS):
                        split_product(dst, lambda s: shid[m][s][:, t * P:(t + 1) * P],
                                      lambda k: down[k][:, NE + m, :], m == 0, False)
                    last = pe.matmul(dst, weight_t[:, t * P:(t + 1) * P], b_out[:], start=False, stop=True)
                last.then_inc(down_psum, 1)

            def batch(b, last=False):
                for c in range(DC):
                    mm = pe.matmul(psum[0:NG, LOGIT_T_BANK, :], wg[:, c, :], ht32[:, c, :],
                                   start=(c == 0), stop=(c == DC - 1))
                mm.then_inc(logit_t_psum, 1)
                pe.wait_ge(ht_split, b + 1)
                up_product(0, 0)
                alone(pe, logit_t_ready, b + 1)
                for t in range(NT):
                    mm = pe.transpose(psum[:, LOGIT_BANK, t * NG:(t + 1) * NG], logit_t[:, t * P:(t + 1) * P],
                                      ident[0:NG, 0:NG])
                mm.then_inc(logit_psum, 1)
                up_product(1, 1)
                for n in range(NE):
                    if n < 2:
                        pe.wait_ge(silu_done, b * HID + n + 1)
                    up_product(NS + 2 * n, n % 2)
                    if n == 1:
                        pe.wait_ge(route, b * ROUTE + 1)
                    up_product(NS + 2 * n + 1, 2 + n % 2)
                    if n == 1:
                        pe.wait_ge(summed, b * DOWN + 1)
                        pe.wait_ge(weight_ready, b * 2 + 2)
                        for t in range(NT):
                            mm = pe.transpose(psum[0:NE + 1, WEIGHT_T_BANK, t * P:(t + 1) * P], weight1[:, t, :], ident[:])
                        mm.then_inc(weight_t_psum, 1)
                    if n >= 1:
                        if n == 2:
                            pe.wait_ge(weight_t_ready, b + 1)
                        if n >= 3:
                            pe.wait_ge(summed, b * DOWN + (n if n == NE - 1 else n - 1))
                        down_product(b, n - 1)
                    if n == NE - 2 and not last:
                        pe.wait_ge(summed, b * DOWN + 4)
                        layer_norm_transposes(b + 1)
                if last:
                    pe.wait_ge(summed, b * DOWN + 4)
                else:
                    pe.wait_ge(ht32_ready, b * DC + 2 * DC)
                shared_down_product(b)
                pe.wait_ge(summed, b * DOWN + NE)
                down_product(b, NE - 1)

            layer_norm_transposes(0)
            pe.wait_ge(up_split, 1)
            pe.wait_ge(ht32_ready, DC)
            pe.wait_ge(small_loaded, 7 * DMA_INC)
            pe.wait_ge(down_split, 1)
            pe.wait_ge(consts, 4)
            with pe.Fori(0, B - 1) as b:
                batch(b)
            batch(B - 1, last=True)


def adaln_block(nc, x, wqk_d, wv_d, wo_d, c_d, wmod_d, up_d, down_d, wg_d, bg_d, bgate_d, bup_d, bsup_d, bdown_d,
                bsdown_d, out):
    B, SEQ, D = x.shape
    x1 = nc.dram_tensor("x1_dram", [B, SEQ, D], F32).ap()
    with ExitStack() as ctx:
        def sb(name, shape):
            return ctx.enter_context(nc.sbuf_tensor(name, shape, F32))

        psum = ctx.enter_context(nc.psum_tensor("psum", [P, 8, 512], F32))
        stage = sb("stage", [P, wo_d.shape[1]])
        mod_t = sb("mod_t", [P, 4 * D // P, B])
        gates = sb("gates", [P, B, 2 * D])
        ident = sb("ident", [P, P])
        up_loaded = ctx.enter_context(nc.semaphore("up_loaded"))
        shared = (nc, psum, stage, mod_t, gates, ident)
        attention_layer(*shared, x, wqk_d, wv_d, wo_d, c_d, wmod_d, up_d, up_loaded, x1)
        feed_forward_layer(*shared, x1, up_loaded, down_d, wg_d, bg_d, bgate_d, bup_d, bsup_d, bdown_d, bsdown_d, out)


def kernel(**inputs):
    import numpy as np
    import concourse.bacc as bacc
    from concourse.bass_utils import run_bass_kernel_spmd

    def get(name):
        return np.asarray(inputs["L0_" + name])

    x = get("attn_x")
    B, SEQ, D = x.shape
    H, E, _ = get("attn_W_Q").shape
    DC = D // P
    NE, _, HID = get("ffn_Wgate").shape
    NS = get("ffn_Ws_up").shape[1] // P

    def qk_layout(w):
        return w.reshape(H, E, DC, P).transpose(3, 0, 2, 1)

    def up_layout(w, n):
        return w.reshape(n, DC, P, HID).transpose(2, 0, 1, 3)

    experts = np.stack([up_layout(get("ffn_Wgate"), NE), up_layout(get("ffn_Wup"), NE)], 2)
    shared = get("ffn_Ws_up").reshape(DC, P, NS, HID).transpose(1, 2, 0, 3)
    arrays = {
        "x": x,
        "wqk": np.stack([qk_layout(get("attn_W_Q")), qk_layout(get("attn_W_K"))], 2).reshape(P, H, 2 * DC * E),
        "wv": get("attn_W_V").reshape(H // 2, 2, E, DC, P).transpose(4, 0, 3, 1, 2).reshape(P, H * DC * E),
        "wo": get("attn_W_O").transpose(2, 0, 1).reshape(P, H * D),
        "c": get("c").reshape(B, DC, P).transpose(2, 1, 0),
        "wmod": get("wmod").reshape(DC, P, 6 * D).transpose(1, 0, 2).reshape(P, DC * 6 * D),
        "up": np.concatenate([shared.reshape(P, -1), experts.reshape(P, -1)], 1),
        "down": np.concatenate([get("ffn_Wdown").transpose(1, 0, 2).reshape(P, -1),
                                get("ffn_Ws_down").reshape(NS, P, D).transpose(1, 0, 2).reshape(P, -1)], 1),
        "wg": get("ffn_Wg").reshape(DC, P, -1).transpose(1, 0, 2),
        "bg": get("ffn_bg").reshape(-1, 1),
        "bgate": get("ffn_bgate").transpose(1, 0),
        "bup": get("ffn_bup").transpose(1, 0),
        "bsup": get("ffn_bs_up").reshape(NS, P).transpose(1, 0),
        "bdown": get("ffn_bdown"),
        "bsdown": get("ffn_bs_down").reshape(1, D),
    }
    nc = bacc.Bacc("TRN2", target_bir_lowering=False, num_devices=1)
    launch, args = {}, []
    for name, a in arrays.items():
        a = np.ascontiguousarray(a)
        launch[f"in_{name}"] = a
        args.append(nc.dram_tensor(f"in_{name}", a.shape, mybir.dt.from_np(a.dtype), kind="ExternalInput").ap())
    args.append(nc.dram_tensor("block_out", x.shape, F32, kind="ExternalOutput").ap())
    adaln_block(nc, *args)
    r = run_bass_kernel_spmd(nc, [launch], core_ids=[0])
    return r.results[0]["block_out"]
```

```python
from contextlib import ExitStack

import concourse.bass as bass
from concourse import mybir

ALU = mybir.AluOpType
ACT = mybir.ActivationFunctionType
AX_X = mybir.AxisListType.X
F32 = mybir.dt.float32
F32R = mybir.dt.float32r

P = 128
DMA_INC = 16
LN_EPS = 1e-5
GATE_MIN = 0.25
MASKED = 1e30
HUGE = 3e38
PASSES = ((0, 0), (0, 1), (1, 0))

S_BANK = ({1: 0, 0: 2, 2: 2, 3: 1}, {1: 4, 0: 5, 2: 5, 3: 3})
S_COL = {1: 0, 0: 0, 2: P, 3: 0}
S_ORDER = (1, 0, 2, 3)
Z_BANK = (3, 1)
QK_BANK = ((4, 5), (0, 2))
V_BANK = (0, 3)
T_BANK = ((1, 2, 0), (3, 4, 5))
ACC_BANK = 6
T_HOLDS = (((0, 0),), ((1, 0), (3, 3 * P)), ((2, 0),))
T_WIDTH = (4 * P, 4 * P, 2 * P)
J_ORDER = (0, 1, 3, 2)
PT_AT = {0: 0, 1: 4 * P, 3: 7 * P, 2: 8 * P}


def tile_at(i):
    return P * (i * (i + 1) // 2)


def alone(eng, semaphore, value):
    eng.wait_ge(semaphore, value)
    eng.nop(nofuse=True)


def rows(dram, b):
    return dram[b].rearrange("(t p) d -> p t d", p=P)


def attention_layer(nc, shared, x, wqk_d, wv_d, wo_d, c_d, wmod_d, up_d, small, x1):
    psum, stage, mod_t, gates, ident, xin, ht32, ht, xres, y, up_loaded, small_loaded, y_free = shared
    B, SEQ, D = x.shape
    H = wo_d.shape[1] // D
    NT = SEQ // P
    DC = D // P
    PAIRS = H // 2
    SW = tile_at(NT)
    HEADS = B * H
    SCALE = 1.0 / float(P) ** 0.5
    CHUNKS = 4
    CHUNK = H * D // CHUNKS

    with ExitStack() as ctx:
        def sb(name, shape, dt=F32):
            return ctx.enter_context(nc.sbuf_tensor(name, shape, dt))

        def sem(name):
            return ctx.enter_context(nc.semaphore(name))

        def pair_of(name, shape):
            return [sb(name + "_hi", shape, F32R), sb(name + "_lo", shape, F32R)]

        wqk = sb("wqk", [P, H + 1, 2 * DC * P])
        wv = pair_of("wv", [P, PAIRS, DC, 2 * P])
        wo = pair_of("wo", [P, H, D])
        ws = pair_of("ws", [P, 2, DC, P])
        stats = sb("stats", [P, NT, 6])
        mv = sb("mv", [P, NT, 2])
        rstd = sb("rstd", [P, NT])
        minus_half = sb("minus_half", [P, NT])
        qt = pair_of("qt", [P, SEQ])
        kt = pair_of("kt", [P, SEQ])
        v = pair_of("v", [P, NT, 2 * P])
        probs = sb("probs", [P, 2, SW])
        pt = pair_of("pt", [P, SW])
        z = pair_of("z", [P, SEQ])
        neg_max = sb("neg_max", [P, 2, NT])
        row_sum = sb("row_sum", [P, 2, NT])
        inv_sum = sb("inv_sum", [P, 2, NT])
        act_c = sb("act_c", [P, DC, B])
        gates8 = sb("gates8", [B, 2 * D])
        gates8s = y[0:B, 0:2, :].rearrange("b t n -> b (t n)")
        gates8a = y[0:B, 2:4, :].rearrange("b t n -> b (t n)")
        mask = sb("mask", [P, SEQ])
        wmod = gates[:].rearrange("p b n -> p (b n)")[:, 0:DC * 6 * D].rearrange("p (c n) -> p c n", c=DC)
        wmod_v = wmod_d.rearrange("p (c n) -> p c n", c=DC)
        gates8_parts = [part[0:B, :] for part in z]

        c_loaded = sem("c_loaded")
        wmod_loaded = sem("wmod_loaded")
        wmod_rest_loaded = sem("wmod_rest_loaded")
        wqk_loaded = sem("wqk_loaded")
        wqk_rest_loaded = sem("wqk_rest_loaded")
        wv_loaded = [sem(f"wv_loaded{k}") for k in range(CHUNKS)]
        wo_loaded = [sem(f"wo_loaded{k}") for k in range(CHUNKS)]
        x_loaded = sem("x_loaded")
        xres_loaded = sem("xres_loaded")
        consts = sem("consts")
        c_act = sem("c_act")
        pick_ready = sem("pick_ready")
        mod_psum = sem("mod_psum")
        mod_ready = sem("mod_ready")
        g8 = sem("g8")
        g8_hi = sem("g8_hi")
        g8_ready = sem("g8_ready")
        gate_psum = sem("gate_psum")
        gate_copied = sem("gate_copied")
        wv_hi = sem("wv_hi")
        wv_split = [sem(f"wv_split{k}") for k in range(CHUNKS)]
        wo_hi = sem("wo_hi")
        wo_split = [sem(f"wo_split{k}") for k in range(CHUNKS)]
        ln_chain = sem("ln_chain")
        ln_var = sem("ln_var")
        ln_rstd = sem("ln_rstd")
        ln_ready = sem("ln_ready")
        ln_psum = sem("ln_psum")
        ht32_ready = sem("ht32_ready")
        ht_hi = sem("ht_hi")
        ht_split = sem("ht_split")
        w_hi = sem("w_hi")
        w_staged = sem("w_staged")
        qk_psum = sem("qk_psum")
        qk_hi = sem("qk_hi")
        qk_split = sem("qk_split")
        v_psum = sem("v_psum")
        v_hi = sem("v_hi")
        v_split = sem("v_split")
        s_psum = sem("s_psum")
        s_masked = sem("s_masked")
        p_exp = sem("p_exp")
        sum_inv = sem("sum_inv")
        p_norm = sem("p_norm")
        p_norm_last = sem("p_norm_last")
        t_psum = sem("t_psum")
        t_hi = sem("t_hi")
        t_split = sem("t_split")
        z_psum = sem("z_psum")
        z_hi = sem("z_hi")
        z_split = sem("z_split")
        o_done = sem("o_done")
        acc_zero = sem("acc_zero")
        acc_gated = sem("acc_gated")
        x1_ready = sem("x1_ready")

        wv_flat = [w[:].rearrange("p a c n -> p (a c n)") for w in wv]
        wo_flat = [w[:].rearrange("p a n -> p (a n)") for w in wo]
        pick = wo_flat[0][0:B, (CHUNKS - 1) * CHUNK:(CHUNKS - 1) * CHUNK + B * P].rearrange("b (n p) -> b n p", n=B)
        acc = psum[:, ACC_BANK:ACC_BANK + 2, :].rearrange("p k (t n) -> p (k t) n", t=2)

        def weights_lo(eng, k, hi, parts, split):
            eng.wait_ge(hi, k + 1)
            at = slice(k * CHUNK, (k + 1) * CHUNK)
            eng.tensor_tensor(parts[1][:, at], stage[:, at], parts[0][:, at], ALU.subtract).then_inc(split[k], 1)

        def ht_split_lo(eng, b, c):
            alone(eng, ht_hi, b + 1)
            eng.tensor_tensor(ht[1][:, c, :], ht32[:, c, :], ht[0][:, c, :], ALU.subtract).then_inc(ht_split, 1)

        def walk(eng, step, batch_begin, last_begin, tail):
            step(0, 0, 0, 0, first=True)
            with eng.Fori(0, B - 1) as b:
                batch_begin(b)
                with eng.Fori(0, PAIRS - 1) as p:
                    step(b * H + p * 2 + 1, p * 2 + 1, 1, b)
                    step(b * H + p * 2 + 2, p * 2 + 2, 0, b, pair=p + 1)
                step(b * H + H - 1, H - 1, 1, b, turn=True)
                step(b * H + H, 0, 0, b + 1, new=True)
            last_begin()
            with eng.Fori(0, PAIRS - 1) as p:
                step(p * 2 + (B - 1) * H + 1, p * 2 + 1, 1, B - 1)
                step(p * 2 + (B - 1) * H + 2, p * 2 + 2, 0, B - 1, pair=p + 1)
            step(HEADS - 1, H - 1, 1, B - 1, last=True)
            tail()

        block = ctx.enter_context(nc.Block())

        @block.sync
        def _(sp):
            sp.dma_start(act_c[:], c_d).then_inc(c_loaded, DMA_INC)
            sp.dma_start(xin[:], rows(x, 0)).then_inc(x_loaded, DMA_INC)
            sp.dma_start(wmod[:, :, 0:2 * D], wmod_v[:, :, 0:2 * D]).then_inc(wmod_loaded, DMA_INC)
            sp.dma_start(wqk[:, 0:2, :], wqk_d[:, 0:2, :]).then_inc(wqk_loaded, DMA_INC)
            sp.dma_start(wmod[:, :, 2 * D:], wmod_v[:, :, 2 * D:]).then_inc(wmod_rest_loaded, DMA_INC)
            sp.dma_start(stage[:, 0:CHUNK], wv_d[:, 0:CHUNK]).then_inc(wv_loaded[0], DMA_INC)
            for k in range(1, CHUNKS):
                sp.dma_start(stage[:, k * CHUNK:(k + 1) * CHUNK], wv_d[:, k * CHUNK:(k + 1) * CHUNK])\
                  .then_inc(wv_loaded[k], DMA_INC)
            sp.dma_start(wqk[:, 2:H, :], wqk_d[:, 2:H, :]).then_inc(wqk_rest_loaded, DMA_INC)
            sp.dma_start(wqk[:, H, :], wqk_d[:, 0, :]).then_inc(wqk_rest_loaded, DMA_INC)
            sp.wait_ge(ln_psum, DC)
            sp.dma_start(xin[:], rows(x, 1)).then_inc(x_loaded, DMA_INC)
            sp.dma_start(xres[:], rows(x, 0)).then_inc(xres_loaded, DMA_INC)
            for k in range(CHUNKS):
                sp.wait_ge(wv_split[k], 1)
                sp.dma_start(stage[:, k * CHUNK:(k + 1) * CHUNK], wo_d[:, k * CHUNK:(k + 1) * CHUNK])\
                  .then_inc(wo_loaded[k], DMA_INC)
            for k in range(CHUNKS):
                sp.wait_ge(wo_split[k], 1)
            sp.dma_start(stage[:, 0:up_d.shape[1]], up_d).then_inc(up_loaded, DMA_INC)
            with sp.Fori(0, B - 2) as b:
                sp.wait_ge(ln_psum, b * DC + 2 * DC)
                sp.dma_start(xin[:], rows(x, b + 2)).then_inc(x_loaded, DMA_INC)
                sp.wait_ge(x1_ready, b + 1)
                sp.dma_start(rows(x1, b), y[:]).then_inc(y_free, DMA_INC)
                sp.dma_start(xres[:], rows(x, b + 1)).then_inc(xres_loaded, DMA_INC)
            sp.wait_ge(ln_psum, B * DC)
            sp.wait_ge(y_free, 2 * DMA_INC)
            sp.dma_start(xin[:], rows(x1, 0)).then_inc(x_loaded, DMA_INC)
            sp.wait_ge(x1_ready, B - 1)
            sp.dma_start(rows(x1, B - 2), y[:]).then_inc(y_free, DMA_INC)
            sp.dma_start(xres[:], rows(x, B - 1)).then_inc(xres_loaded, DMA_INC)
            for dst, src in small:
                sp.dma_start(dst, src).then_inc(small_loaded, DMA_INC)
            sp.wait_ge(x1_ready, B)
            sp.dma_start(rows(x1, B - 1), y[:]).then_inc(y_free, DMA_INC)

        @block.gpsimd
        def _(pool):
            pool.memset(ident[:], 0.0).then_inc(consts, 1)
            pool.memset(mask[:], 0.0).then_inc(consts, 1)
            pool.wait_ge(consts, 2)
            pool.affine_select(out=ident[:], in_=ident[:], compare_op=ALU.not_equal, fill=1.0, base=0,
                               pattern=[[-1, P]], channel_multiplier=1).then_inc(consts, 1)
            pool.affine_select(out=mask[:, SEQ - P:], in_=mask[:, SEQ - P:], compare_op=ALU.is_ge, fill=MASKED,
                               base=0, pattern=[[-1, P]], channel_multiplier=1).then_inc(consts, 1)
            pool.memset(minus_half[:], -0.5).then_inc(consts, 1)
            pool.wait_ge(consts, 5)

            def layer_norm_rstd(b):
                pool.wait_ge(ln_var, b + 1)
                pool.tensor_tensor(rstd[:], mv[:, :, 1], minus_half[:], ALU.pow).then_inc(ln_rstd, 1)

            def stage_weights(i, h):
                if not (isinstance(i, int) and i == 0):
                    alone(pool, qk_psum, i * 2)
                src = wqk[:, h, :].rearrange("p (a c e) -> p a c e", a=2, c=DC)
                pool.tensor_copy(ws[0][:], src).then_inc(w_hi, 1)
                alone(pool, w_hi, i + 1)
                pool.tensor_tensor(ws[1][:], src, ws[0][:], ALU.subtract).then_inc(w_staged, 1)

            layer_norm_rstd(0)
            pool.wait_ge(wqk_loaded, DMA_INC)
            stage_weights(0, 0)
            ht_split_lo(pool, 0, 1)
            stage_weights(1, 1)

            def step(i, h, odd, b, pair=0, first=False, turn=False, new=False, last=False):
                if turn:
                    ht_split_lo(pool, b + 1, 1)
                alone(pool, sum_inv, i * 2 + 1)
                for t in S_ORDER[:-1]:
                    row = probs[:, odd, tile_at(t):tile_at(t + 1)]
                    pool.tensor_scalar(row, row, inv_sum[:, odd, t:t + 1], 1.0, ALU.mult, ALU.mult).then_inc(p_norm, 1)
                if new:
                    add_residual(b - 1)
                if first:
                    weights_lo(pool, 2, wv_hi, wv_flat, wv_split)
                    pool.wait_ge(wqk_rest_loaded, 2 * DMA_INC)
                if not last:
                    stage_weights(i + 2, 1 if turn else h + 2)
                if last:
                    ht_split_lo(pool, B, 1)
                if turn:
                    layer_norm_rstd(b + 2)
                if first:
                    layer_norm_rstd(1)
                    for k in (0, 1):
                        weights_lo(pool, k, wo_hi, wo_flat, wo_split)

            def add_residual(b):
                pool.wait_ge(acc_gated, b + 2)
                pool.wait_ge(xres_loaded, b * DMA_INC + DMA_INC)
                pool.tensor_tensor(y[:], y[:], xres[:], ALU.add).then_inc(x1_ready, 1)

            walk(pool, step, lambda b: None, lambda: None, lambda: None)

        @block.scalar
        def _(act):
            act.wait_ge(c_loaded, DMA_INC)
            act.activation(act_c[:], act_c[:], ACT.Silu).then_inc(c_act, 1)
            act.wait_ge(consts, 3)
            act.activation(pick, ident[0:B, 0:B].rearrange("b (n p) -> b n p", p=1).to_broadcast([B, B, P]),
                           ACT.Copy).then_inc(pick_ready, 1)

            def ht_evacuate(b):
                for c in range(DC):
                    act.wait_ge(ln_psum, b * DC + c + 1)
                    act.activation(ht32[:, c, :], psum[:, ACC_BANK + c, :], ACT.Identity,
                                   bias=mod_t[:, c, bass.ds(b, 1)],
                                   scale=mod_t[:, DC + c, bass.ds(b, 1)]).then_inc(ht32_ready, 1)

            def ht_split_hi(b):
                act.wait_ge(ht32_ready, b * DC + DC)
                act.activation(ht[0][:], ht32[:], ACT.Copy).then_inc(ht_hi, 1)

            def qk_evacuate(i, odd):
                for n, dst in enumerate((qt, kt)):
                    act.wait_ge(qk_psum, i * 2 + n + 1)
                    act.activation(dst[0][:], psum[:, QK_BANK[1 - odd][n], :], ACT.Copy,
                                   scale=(-SCALE, 1.0)[n]).then_inc(qk_hi, 1)

            act.wait_ge(consts, 5)
            act.wait_ge(mod_ready, 1)
            ht_evacuate(0)
            ht_split_hi(0)
            qk_evacuate(0, 0)
            act.wait_ge(g8, 5)
            act.activation(gates8_parts[0], gates8[:], ACT.Copy).then_inc(g8_hi, 1)

            def weights_hi(k, loaded, dst, done):
                act.wait_ge(loaded[k], DMA_INC)
                act.activation(dst[:, k * CHUNK:(k + 1) * CHUNK], stage[:, k * CHUNK:(k + 1) * CHUNK],
                               ACT.Copy).then_inc(done, 1)

            weights_hi(0, wv_loaded, wv_flat[0], wv_hi)

            def step(i, h, odd, b, pair=0, first=False, turn=False, new=False, last=False):
                if turn:
                    act.wait_ge(v_psum, b * H + H)
                    act.wait_ge(qk_psum, b * 2 * H + 2 * H)
                    ht_split_hi(b + 1)
                for n, t in enumerate(S_ORDER):
                    if n == NT - 1 and not first:
                        z_evacuate(i - 1, 1 - odd)
                    act.wait_ge(s_masked, i * NT + n + 1)
                    row = probs[:, odd, tile_at(t):tile_at(t + 1)]
                    act.activation(row, row, ACT.Exp, bias=neg_max[:, odd, t:t + 1], scale=-1.0,
                                   accum_out=row_sum[:, odd, t:t + 1]).then_inc(p_exp, 1)
                if not last:
                    qk_evacuate(i + 1, 1 - odd)
                else:
                    next_layers_ht()
                if not odd:
                    for half in range(2):
                        act.wait_ge(v_psum, i + half + 1)
                        act.activation(v[0][:, 2 * half:2 * half + 2, :].rearrange("p t n -> p (t n)"),
                                       psum[:, V_BANK[half], :], ACT.Copy).then_inc(v_hi, 1)
                if first:
                    for k in (1, 2):
                        weights_hi(k, wv_loaded, wv_flat[0], wv_hi)
                for n in range(3):
                    act.wait_ge(t_psum, i * 3 + n + 1)
                    act.activation(pt[0][:, n * 4 * P:n * 4 * P + T_WIDTH[n]],
                                   psum[:, T_BANK[odd][n], 0:T_WIDTH[n]], ACT.Copy).then_inc(t_hi, 1)
                if first:
                    weights_hi(3, wv_loaded, wv_flat[0], wv_hi)
                    for n in range(B):
                        act.wait_ge(gate_psum, n + 1)
                        act.activation(gates[:, n, :], psum[:, ACC_BANK + n % 2, :], ACT.Copy)\
                           .then_inc(gate_copied, 1)
                        if n == B // 2:
                            weights_hi(0, wo_loaded, wo_flat[0], wo_hi)
                    for k in range(1, CHUNKS):
                        weights_hi(k, wo_loaded, wo_flat[0], wo_hi)

            def next_layers_ht():
                act.wait_ge(mod_ready, 2)
                for c in range(DC):
                    act.wait_ge(ln_psum, B * DC + c + 1)
                    act.activation(ht32[:, c, :], psum[:, QK_BANK[1][c], :], ACT.Identity,
                                   bias=mod_t[:, 2 * DC + c, 0:1],
                                   scale=mod_t[:, 3 * DC + c, 0:1]).then_inc(ht32_ready, 1)
                ht_split_hi(B)

            def z_evacuate(i, odd):
                act.wait_ge(z_psum, i + 1)
                act.activation(z[0][:], psum[:, Z_BANK[1 - odd], :], ACT.Copy).then_inc(z_hi, 1)

            def zero_acc(k):
                act.activation(psum[:, ACC_BANK + k, :], mask[:, 0:1].to_broadcast([P, SEQ]), ACT.Copy).then_inc(acc_zero, 1)

            def batch_begin(b):
                ht_evacuate(b + 1)
                for k in range(2):
                    act.wait_ge(ht32_ready, (b + 1) * DC + k + 1)
                    zero_acc(k)

            def last_begin():
                act.wait_ge(acc_gated, B)
                for k in range(2):
                    zero_acc(k)

            walk(act, step, batch_begin, last_begin, lambda: z_evacuate(HEADS - 1, 1))

        @block.vector
        def _(dve):
            def layer_norm_statistics(b):
                dve.wait_ge(x_loaded, b * DMA_INC + DMA_INC)
                for t in range(NT):
                    dve.bn_stats(stats[:, t, :], xin[:, t, :]).then_inc(ln_chain, 1)
                alone(dve, ln_chain, b * 2 * NT + NT)
                for t in range(NT):
                    dve.bn_aggr(mv[:, t, :], stats[:, t, :]).then_inc(ln_chain, 1)
                dve.wait_ge(ln_chain, b * 2 * NT + 2 * NT)
                dve.tensor_scalar(mv[:, :, 1], mv[:, :, 1], LN_EPS, None, ALU.add).then_inc(ln_var, 1)

            def layer_norm_apply(b):
                dve.wait_ge(ln_rstd, b + 1)
                for t in range(NT):
                    last = dve.tensor_scalar(xin[:, t, :], xin[:, t, :], mv[:, t, 0:1], rstd[:, t:t + 1],
                                             ALU.subtract, ALU.mult)
                last.then_inc(ln_ready, 1)

            def qk_lo(i, odd):
                for n, dst in enumerate((qt, kt)):
                    dve.wait_ge(qk_hi, i * 2 + n + 1)
                    dve.scalar_tensor_tensor(out=dst[1][:], in0=psum[:, QK_BANK[1 - odd][n], :],
                                             scalar=(-SCALE, 1.0)[n], in1=dst[0][:], op0=ALU.mult,
                                             op1=ALU.subtract).then_inc(qk_split, 1)

            dve.sem_inc(y_free, DMA_INC)
            dve.sem_inc(acc_gated, 1)
            layer_norm_statistics(0)
            layer_norm_apply(0)

            def shift_and_scale(k, bank):
                src = psum[:, bank, 0:2 * DC * B].rearrange("p (k b) -> p k b", b=B)
                at = 2 * k * DC
                dve.tensor_copy(mod_t[:, at:at + DC, :], src[:, 0:DC, :])
                return dve.tensor_scalar(mod_t[:, at + DC:at + 2 * DC, :], src[:, DC:, :], 1.0, None, ALU.add)

            dve.wait_ge(mod_psum, 1)
            shift_and_scale(0, 0).then_inc(mod_ready, 1)
            ht_split_lo(dve, 0, 0)
            dve.wait_ge(mod_psum, 2)
            shift_and_scale(1, 1).then_inc(mod_ready, 1)
            dve.wait_ge(mod_psum, 3)
            dve.tensor_copy(gates8[:], psum[0:B, 3, :]).then_inc(g8, 1)
            dve.wait_ge(g8, 1)
            dve.tensor_scalar(gates8s, gates8[:], 0.0, 2.0, ALU.is_ge, ALU.mult).then_inc(g8, 1)
            dve.scalar_tensor_tensor(out=gates8a, in0=gates8[:], scalar=-1.0, in1=gates8[:],
                                     op0=ALU.mult, op1=ALU.max).then_inc(g8, 1)
            dve.wait_ge(g8, 3)
            dve.tensor_scalar(gates8a, gates8a, GATE_MIN, None, ALU.max).then_inc(g8, 1)
            dve.wait_ge(g8, 4)
            dve.scalar_tensor_tensor(out=gates8[:], in0=gates8s, scalar=-1.0, in1=gates8a,
                                     op0=ALU.add, op1=ALU.mult).then_inc(g8, 1)
            qk_lo(0, 0)
            dve.wait_ge(g8_hi, 1)
            dve.tensor_tensor(gates8_parts[1], gates8[:], gates8_parts[0], ALU.subtract).then_inc(g8_ready, 1)

            weights_lo(dve, 0, wv_hi, wv_flat, wv_split)

            def z_lo(i, odd):
                dve.wait_ge(z_hi, i + 1)
                dve.tensor_tensor(z[1][:], psum[:, Z_BANK[1 - odd], :], z[0][:], ALU.subtract).then_inc(z_split, 1)

            def gate_output(b):
                dve.wait_ge(o_done, b * H + H)
                dve.wait_ge(y_free, b * DMA_INC + DMA_INC)
                for k in range(2):
                    last = dve.tensor_tensor(
                        y[:, 2 * k:2 * k + 2, :], acc[:, 2 * k:2 * k + 2, :],
                        gates[:, bass.ds(b, 1), 0:D].to_broadcast([P, 2, D]), ALU.mult)
                last.then_inc(acc_gated, 1)

            def step(i, h, odd, b, pair=0, first=False, turn=False, new=False, last=False):
                if turn:
                    ht_split_lo(dve, b + 1, 0)
                for n, t in enumerate(S_ORDER):
                    alone(dve, s_psum, i * 3 + (1, 2, 2, 3)[n])
                    width = P * (t + 1)
                    dve.tensor_tensor_reduce(
                        out=probs[:, odd, tile_at(t):tile_at(t + 1)],
                        in0=psum[:, S_BANK[odd][t], S_COL[t]:S_COL[t] + width], in1=mask[:, SEQ - width:],
                        scale=1.0, scalar=HUGE, op0=ALU.add, op1=ALU.min,
                        accum_out=neg_max[:, odd, t:t + 1]).then_inc(s_masked, 1)
                dve.wait_ge(p_exp, i * NT + NT - 1)
                dve.reciprocal(inv_sum[:, odd, 0:NT - 1], row_sum[:, odd, 0:NT - 1]).then_inc(sum_inv, 1)
                if not first:
                    z_lo(i - 1, 1 - odd)
                dve.wait_ge(p_exp, i * NT + NT)
                dve.reciprocal(inv_sum[:, odd, NT - 1:], row_sum[:, odd, NT - 1:]).then_inc(sum_inv, 1)
                dve.wait_ge(sum_inv, i * 2 + 2)
                row = probs[:, odd, tile_at(NT - 1):]
                dve.tensor_scalar(row, row, inv_sum[:, odd, NT - 1:], None, ALU.mult).then_inc(p_norm_last, 1)
                if not last:
                    qk_lo(i + 1, 1 - odd)
                else:
                    ht_split_lo(dve, B, 0)
                if turn:
                    layer_norm_statistics(b + 2)
                if new:
                    gate_output(b - 1)
                    layer_norm_apply(b + 1)
                if not odd:
                    for half in range(2):
                        dve.wait_ge(v_hi, i + half + 1)
                        out = v[1][:, 2 * half:2 * half + 2, :].rearrange("p t n -> p (t n)")
                        hi = v[0][:, 2 * half:2 * half + 2, :].rearrange("p t n -> p (t n)")
                        dve.tensor_tensor(out, psum[:, V_BANK[half], :], hi, ALU.subtract).then_inc(v_split, 1)
                for n in range(3):
                    dve.wait_ge(t_hi, i * 3 + n + 1)
                    at = slice(n * 4 * P, n * 4 * P + T_WIDTH[n])
                    dve.tensor_tensor(pt[1][:, at], psum[:, T_BANK[odd][n], 0:T_WIDTH[n]], pt[0][:, at],
                                      ALU.subtract).then_inc(t_split, 1)
                if first:
                    for k in (1, 3):
                        weights_lo(dve, k, wv_hi, wv_flat, wv_split)
                    layer_norm_statistics(1)
                    layer_norm_apply(1)
                    for k in (2, 3):
                        weights_lo(dve, k, wo_hi, wo_flat, wo_split)

            def tail():
                z_lo(HEADS - 1, 1)
                gate_output(B - 1)
                dve.wait_ge(acc_gated, B + 1)
                dve.wait_ge(xres_loaded, B * DMA_INC)
                dve.tensor_tensor(y[:], y[:], xres[:], ALU.add).then_inc(x1_ready, 1)

            walk(dve, step, lambda b: None, lambda: None, tail)

        @block.tensor
        def _(pe):
            def split_product(out, stationary, moving, start, stop, skip=False):
                for n, (s, m) in enumerate(PASSES):
                    last = pe.matmul(out, stationary(s), moving(m), start=start and n == 0,
                                     stop=stop and n == len(PASSES) - 1, skip_group_check=skip)
                return last

            def layer_norm_transposes(b, banks=(ACC_BANK, ACC_BANK + 1)):
                pe.wait_ge(ln_ready, b + 1)
                for c in range(DC):
                    for t in range(NT):
                        last = pe.transpose(psum[:, banks[c], t * P:(t + 1) * P],
                                            xin[:, t, c * P:(c + 1) * P], ident[:])
                    last.then_inc(ln_psum, 1)

            def queries_keys(i, odd):
                pe.wait_ge(w_staged, i + 1)
                for n in range(2):
                    for c in range(DC):
                        last = split_product(psum[:, QK_BANK[1 - odd][n], :], lambda s: ws[s][:, n, c, :],
                                             lambda m: ht[m][:, c, :], c == 0, c == DC - 1)
                    last.then_inc(qk_psum, 1)

            def modulation(first_cols, bank):
                at = 0
                for first_col in first_cols:
                    for col in range(first_col, first_col + D, P):
                        for c in range(DC):
                            last = pe.matmul(psum[:, bank, at:at + B], wmod[:, c, col:col + P], act_c[:, c, :],
                                             start=(c == 0), stop=(c == DC - 1))
                        at += B
                last.then_inc(mod_psum, 1)

            pe.wait_ge(c_act, 1)
            pe.wait_ge(wmod_loaded, DMA_INC)
            modulation((0, D), 0)
            pe.wait_ge(consts, 5)
            layer_norm_transposes(0)
            pe.wait_ge(wmod_rest_loaded, DMA_INC)
            modulation((3 * D, 4 * D), 1)
            for k in range(2):
                for c in range(DC):
                    last = pe.matmul(psum[0:B, 3, k * D:(k + 1) * D], act_c[:, c, :],
                                     wmod[:, c, (3 * k + 2) * D:(3 * k + 3) * D],
                                     start=(c == 0), stop=(c == DC - 1))
            last.then_inc(mod_psum, 1)

            pe.wait_ge(ht_split, DC)
            queries_keys(0, 0)

            def gates_to_all():
                pe.wait_ge(pick_ready, 1)
                pe.wait_ge(g8_ready, 1)
                for b in range(B):
                    if b >= 2:
                        pe.wait_ge(gate_copied, b - 1)
                    for n, part in enumerate(gates8_parts):
                        last = pe.matmul(psum[:, ACC_BANK + b % 2, :], pick[:, b, :], part,
                                         start=(n == 0), stop=(n == 1))
                    last.then_inc(gate_psum, 1)
                pe.wait_ge(gate_copied, B)

            def scores(i, odd):
                pe.wait_ge(qk_split, i * 2 + 2)
                for n, t in enumerate(S_ORDER):
                    if t == 3:
                        if odd:
                            pe.wait_ge(v_split, i + 1)
                    width = P * (t + 1)
                    last = split_product(psum[:, S_BANK[odd][t], S_COL[t]:S_COL[t] + width],
                                         lambda s: qt[s][:, t * P:(t + 1) * P], lambda m: kt[m][:, 0:width],
                                         True, True)
                    if t != 0:
                        last.then_inc(s_psum, 1)

            def weighted_values(i, odd):
                for n, j in enumerate(J_ORDER):
                    if n != 2:
                        pe.wait_ge(t_split, i * 3 + (1, 2, 0, 3)[n])
                    width = SEQ - P * j
                    last = split_product(psum[:, Z_BANK[1 - odd], P * j:], lambda s: v[s][:, j, odd * P:(odd + 1) * P],
                                         lambda m: pt[m][:, PT_AT[j]:PT_AT[j] + width], n == 0, n == NT - 1)
                last.then_inc(z_psum, 1)

            def project(i, h):
                pe.wait_ge(z_split, i + 1)
                for t in range(NT):
                    last = split_product(acc[:, t, :], lambda s: z[s][:, t * P:(t + 1) * P],
                                         lambda m: wo[m][:, h, :], False, True, skip=True)
                last.then_inc(o_done, 1)

            def values(i, pair):
                pe.wait_ge(s_masked, i * NT + 1)
                for t in range(NT):
                    for c in range(DC):
                        last = split_product(psum[:, V_BANK[t // 2], (t % 2) * 2 * P:(t % 2 + 1) * 2 * P],
                                             lambda s: ht[s][:, c, t * P:(t + 1) * P],
                                             lambda m: wv[m][:, pair, c, :], c == 0, c == DC - 1)
                    if t % 2:
                        last.then_inc(v_psum, 1)

            def transposes(i, odd):
                pe.wait_ge(p_norm, i * (NT - 1) + NT - 1)
                for tiles in (range(NT - 1), range(NT - 1, NT)):
                    if NT - 1 in tiles:
                        pe.wait_ge(p_norm_last, i + 1)
                    for n, held in enumerate(T_HOLDS):
                        if not odd and n == 2 and NT - 1 not in tiles:
                            pe.wait_ge(v_split, i + 1)
                        for j, col in held:
                            for t in tiles:
                                if t >= j:
                                    last = pe.transpose(
                                        psum[:, T_BANK[odd][n], col + (t - j) * P:col + (t - j + 1) * P],
                                        probs[:, odd, tile_at(t) + j * P:tile_at(t) + (j + 1) * P], ident[:])
                        if NT - 1 in tiles:
                            last.then_inc(t_psum, 1)

            def step(i, h, odd, b, pair=0, first=False, turn=False, new=False, last=False):
                scores(i, odd)
                if not first:
                    weighted_values(i - 1, 1 - odd)
                if turn:
                    pe.wait_ge(ht_split, b * DC + 2 * DC)
                if not last:
                    queries_keys(i + 1, 1 - odd)
                else:
                    layer_norm_transposes(B, QK_BANK[1])
                if not first:
                    if not new:
                        pe.wait_ge(acc_zero, b * 2 + 2)
                    if odd:
                        for k in range(CHUNKS):
                            pe.wait_ge(wo_split[k], 1)
                    project(i - 1, H - 1 if new else h - 1)
                if not odd:
                    for k in range(1 if first else CHUNKS):
                        pe.wait_ge(wv_split[k], 1)
                    values(i, pair)
                transposes(i, odd)
                if first:
                    gates_to_all()

            def batch_begin(b):
                pe.wait_ge(acc_gated, b + 1)
                layer_norm_transposes(b + 1)

            def tail():
                weighted_values(HEADS - 1, 1)
                project(HEADS - 1, H - 1)

            walk(pe, step, batch_begin, lambda: None, tail)


def feed_forward_layer(nc, shared, small, x1, down_d, out):
    psum, stage, mod_t, gates, ident, xin, ht32, ht, xres, y, up_loaded, small_loaded, attention_y_free = shared
    wg, bg, b_gate, b_up, b_sup, b_out = small
    B, SEQ, D = x1.shape
    NT = SEQ // P
    DC = D // P
    NE = b_gate.shape[1]
    NS = b_sup.shape[1]
    NG = wg.shape[2]
    KEPT = NE
    UPS = NS + 2 * NE
    UP, HID, DOWN = NS + 2 * NE, NS + NE, NE + 1
    ROUTE = 9
    Y_BANK = (4, 6)
    LOGIT_T_BANK, LOGIT_BANK, WEIGHT_T_BANK = 2, 3, 6

    with ExitStack() as ctx:
        def sb(name, shape, dt=F32):
            return ctx.enter_context(nc.sbuf_tensor(name, shape, dt))

        def sem(name):
            return ctx.enter_context(nc.semaphore(name))

        def pair_of(name, shape):
            return [sb(name + "_hi", shape, F32R), sb(name + "_lo", shape, F32R)]

        up = pair_of("f_up", [P, UPS, DC, P])
        down_raw = sb("f_down_raw", [P, NE + NS, D])
        down = pair_of("f_down", [P, NE + NS, D])
        minus_half = sb("f_minus_half", [P, NT])
        earlier = sb("f_earlier", [P, NG, NG])
        stats = sb("f_stats", [P, NT, 6])
        mv = sb("f_mv", [P, NT, 2])
        rstd = sb("f_rstd", [P, NT])
        logit_t = sb("f_logit_t", [NG, SEQ])
        logit = sb("f_logit", [P, NT, NG])
        top = sb("f_top", [P, NT])
        above = sb("f_above", [P, NT, NG, NG])
        equal = sb("f_equal", [P, NT, NG, NG])
        rank = sb("f_rank", [P, NT, NG])
        kept = sb("f_kept", [P, NT, NG])
        shifted = sb("f_shifted", [P, NT, NG])
        weight = sb("f_weight", [P, NT, NG])
        total = sb("f_total", [P, NT])
        inv_total = sb("f_inv_total", [P, NT])
        weight1 = sb("f_weight1", [P, NT, NE + 1])
        weight_t = sb("f_weight_t", [NE + 1, SEQ])
        gated = sb("f_gated", [P, 2, SEQ])
        hid32 = sb("f_hid32", [P, 2, SEQ])
        hid = [pair_of(f"f_hid{n}", [P, SEQ]) for n in range(2)]
        shid32 = sb("f_shid32", [P, NS, SEQ])
        shid = [pair_of(f"f_shid{n}", [P, SEQ]) for n in range(NS)]
        f = sb("f_sum", [P, NT, D])

        down_loaded = [sem(f"f_down_loaded{k}") for k in range(2)]
        x_loaded = sem("f_x_loaded")
        xres_loaded = sem("f_xres_loaded")
        y_free = sem("f_y_free")
        consts = sem("f_consts")
        up_hi = sem("f_up_hi")
        up_split = sem("f_up_split")
        down_hi = sem("f_down_hi")
        down_split = sem("f_down_split")
        ln_chain = sem("f_ln_chain")
        ln_var = sem("f_ln_var")
        ln_rstd = sem("f_ln_rstd")
        ln_ready = sem("f_ln_ready")
        ln_psum = sem("f_ln_psum")
        ht32_ready = sem("f_ht32_ready")
        ht_hi = sem("f_ht_hi")
        ht_split = sem("f_ht_split")
        logit_t_psum = sem("f_logit_t_psum")
        logit_t_ready = sem("f_logit_t_ready")
        logit_psum = sem("f_logit_psum")
        route = sem("f_route")
        shifted_ready = sem("f_shifted_ready")
        weight_exp = sem("f_weight_exp")
        weight_ready = sem("f_weight_ready")
        weight_t_psum = sem("f_weight_t_psum")
        weight_t_ready = sem("f_weight_t_ready")
        up_psum = sem("f_up_psum")
        silu_done = sem("f_silu_done")
        glu_done = sem("f_glu_done")
        hid_hi = sem("f_hid_hi")
        hid_split = sem("f_hid_split")
        shid_split = sem("f_shid_split")
        down_psum = sem("f_down_psum")
        summed = sem("f_summed")
        f_read = sem("f_f_read")
        y_ready = sem("f_y_ready")
        last_gated = sem("f_last_gated")

        up_flat = [w[:].rearrange("p a c n -> p (a c n)") for w in up]
        down_flat = [w[:].rearrange("p a n -> p (a n)") for w in down]
        down_raw_flat = down_raw[:].rearrange("p a n -> p (a n)")
        UP_ENDS = (NS, NS + 4, UPS)
        UP_CHUNKS = [slice(a * DC * P, e * DC * P) for a, e in zip((0,) + UP_ENDS, UP_ENDS)]
        DOWN_CHUNK = (NE + NS) * D // 2

        def y_bank(k):
            return psum[:, Y_BANK[k]:Y_BANK[k] + 2, :].rearrange("p k (t n) -> p (k t) n", t=2)

        block = ctx.enter_context(nc.Block())

        @block.sync
        def _(sp):
            for k in range(2):
                sp.dma_start(down_raw_flat[:, k * DOWN_CHUNK:(k + 1) * DOWN_CHUNK],
                             down_d[:, k * DOWN_CHUNK:(k + 1) * DOWN_CHUNK]).then_inc(down_loaded[k], DMA_INC)
            sp.dma_start(xin[:], rows(x1, 1)).then_inc(x_loaded, DMA_INC)
            sp.wait_ge(attention_y_free, DMA_INC * B + DMA_INC)
            sp.sem_inc(y_free, DMA_INC)
            with sp.Fori(0, B - 2) as b:
                sp.dma_start(xres[:], rows(x1, b)).then_inc(xres_loaded, DMA_INC)
                sp.wait_ge(ln_psum, b * DC + DC)
                sp.dma_start(xin[:], rows(x1, b + 2)).then_inc(x_loaded, DMA_INC)
                sp.wait_ge(y_ready, b + 1)
                sp.dma_start(rows(out, b), y[:]).then_inc(y_free, DMA_INC)
            sp.dma_start(xres[:], rows(x1, B - 2)).then_inc(xres_loaded, DMA_INC)
            sp.wait_ge(y_ready, B - 1)
            sp.dma_start(rows(out, B - 2), y[:]).then_inc(y_free, DMA_INC)
            sp.dma_start(xres[:], rows(x1, B - 1)).then_inc(xres_loaded, DMA_INC)
            for k in range(2):
                at = slice(k * NT // 2, (k + 1) * NT // 2)
                sp.wait_ge(y_ready, B + k)
                sp.dma_start(rows(out, B - 1)[:, at, :], y[:, at, :]).then_inc(y_free, DMA_INC)
            sp.wait_ge(y_free, B * DMA_INC + 2 * DMA_INC)

        @block.gpsimd
        def _(pool):
            pool.memset(minus_half[:], -0.5).then_inc(consts, 1)
            pool.memset(earlier[:], 1.0).then_inc(consts, 1)
            pool.memset(weight1[:], 1.0).then_inc(consts, 1)
            pool.wait_ge(consts, 3)
            pool.affine_select(out=earlier[:], in_=earlier[:], compare_op=ALU.is_ge, fill=0.0, base=-1,
                               pattern=[[1, NG], [-1, NG]], channel_multiplier=0).then_inc(consts, 1)

            def layer_norm_rstd(b):
                pool.wait_ge(ln_var, b + 1)
                pool.tensor_tensor(rstd[:], mv[:, :, 1], minus_half[:], ALU.pow).then_inc(ln_rstd, 1)

            def ht_split_lo(b):
                pool.wait_ge(ht_hi, b + 1)
                pool.tensor_tensor(ht[1][:], ht32[:], ht[0][:], ALU.subtract).then_inc(ht_split, 1)

            def shared_lo(b):
                for m in range(NS):
                    pool.wait_ge(hid_hi, b * HID + m + 1)
                    pool.tensor_tensor(shid[m][1][:], shid32[:, m, :], shid[m][0][:], ALU.subtract).then_inc(shid_split, 1)

            def finish(b):
                pool.wait_ge(summed, b * DOWN + DOWN + 1)
                alone(pool, y_free, b * DMA_INC + DMA_INC)
                gate = gates[:, bass.ds(b, 1), D:2 * D].to_broadcast([P, NT, D])
                pool.tensor_tensor(y[:], f[:], gate, ALU.mult).then_inc(f_read, 1)
                pool.wait_ge(xres_loaded, b * DMA_INC + DMA_INC)
                alone(pool, f_read, b + 2)
                pool.tensor_tensor(y[:], y[:], xres[:], ALU.add).then_inc(y_ready, 1)

            for k in range(2):
                pool.wait_ge(down_hi, k + 1)
                at = slice(k * DOWN_CHUNK, (k + 1) * DOWN_CHUNK)
                pool.tensor_tensor(down_flat[1][:, at], down_raw_flat[:, at], down_flat[0][:, at],
                                   ALU.subtract).then_inc(down_split, 1)
            with pool.Fori(0, B - 1) as b:
                shared_lo(b)
                layer_norm_rstd(b)
                ht_split_lo(b)
                finish(b)
            shared_lo(B - 1)

        @block.scalar
        def _(act):
            def ht_evacuate(b):
                for c in range(DC):
                    act.wait_ge(ln_psum, b * DC + c + 1)
                    act.activation(ht32[:, c, :], psum[:, Y_BANK[0] + c, :], ACT.Identity,
                                   bias=mod_t[:, 2 * DC + c, bass.ds(b + 1, 1)],
                                   scale=mod_t[:, 3 * DC + c, bass.ds(b + 1, 1)]).then_inc(ht32_ready, 1)

            def ht_split_hi(b):
                act.wait_ge(ht32_ready, b * DC + DC)
                act.activation(ht[0][:], ht32[:], ACT.Copy).then_inc(ht_hi, 1)

            act.wait_ge(up_loaded, DMA_INC)
            for at in UP_CHUNKS:
                act.activation(up_flat[0][:, at], stage[:, at], ACT.Copy).then_inc(up_hi, 1)
            for k in range(2):
                act.wait_ge(down_loaded[k], DMA_INC)
                at = slice(k * DOWN_CHUNK, (k + 1) * DOWN_CHUNK)
                act.activation(down_flat[0][:, at], down_raw_flat[:, at], ACT.Copy).then_inc(down_hi, 1)
            act.wait_ge(small_loaded, len(small) * DMA_INC + DMA_INC)

            def hi(b, n, dst, src):
                act.activation(dst[0][:], src, ACT.Copy).then_inc(hid_hi, 1)

            def batch(b, last=False):
                for m in range(NS):
                    act.wait_ge(up_psum, b * UP + m + 1)
                    act.activation(shid32[:, m, :], psum[:, m, :], ACT.Silu,
                                   bias=b_sup[:, m:m + 1]).then_inc(silu_done, 1)
                    act.wait_ge(silu_done, b * HID + m + 1)
                    hi(b, m, shid[m], shid32[:, m, :])
                for n in range(NE):
                    act.wait_ge(up_psum, b * UP + NS + 2 * n + 1)
                    act.activation(gated[:, n % 2, :], psum[:, n % 2, :], ACT.Silu,
                                   bias=b_gate[:, n:n + 1]).then_inc(silu_done, 1)
                    if n == 0:
                        act.wait_ge(shifted_ready, b + 1)
                        act.activation(weight[:], shifted[:], ACT.Exp).then_inc(weight_exp, 1)
                    act.wait_ge(glu_done, b * NE + n + 1)
                    hi(b, NS + n, hid[n % 2], hid32[:, n % 2, :])
                    if n == 1:
                        act.wait_ge(weight_t_psum, b + 1)
                        act.activation(weight_t[:], psum[0:NE + 1, WEIGHT_T_BANK, :], ACT.Copy).then_inc(weight_t_ready, 1)
                    if n == NE - 2 and not last:
                        ht_evacuate(b)
                if not last:
                    act.wait_ge(up_psum, b * UP + UP)
                    ht_split_hi(b)

            with act.Fori(0, B - 1) as b:
                batch(b)
            batch(B - 1, last=True)

        @block.vector
        def _(dve):
            def layer_norm_sums(b):
                dve.wait_ge(x_loaded, b * DMA_INC + DMA_INC)
                for t in range(NT):
                    dve.bn_stats(stats[:, t, :], xin[:, t, :]).then_inc(ln_chain, 1)

            def layer_norm_statistics(b):
                alone(dve, ln_chain, b * 2 * NT + NT)
                for t in range(NT):
                    dve.bn_aggr(mv[:, t, :], stats[:, t, :]).then_inc(ln_chain, 1)
                dve.wait_ge(ln_chain, b * 2 * NT + 2 * NT)
                dve.tensor_scalar(mv[:, :, 1], mv[:, :, 1], LN_EPS, None, ALU.add).then_inc(ln_var, 1)

            def layer_norm_apply(b):
                dve.wait_ge(ln_rstd, b + 1)
                for t in range(NT):
                    last = dve.tensor_scalar(xin[:, t, :], xin[:, t, :], mv[:, t, 0:1], rstd[:, t:t + 1],
                                             ALU.subtract, ALU.mult)
                last.then_inc(ln_ready, 1)

            LAYER_NORM_PARTS = (layer_norm_sums, layer_norm_statistics, layer_norm_apply)

            dve.sem_inc(summed, 1)
            dve.sem_inc(f_read, 1)
            dve.sem_inc(ht_split, 1)
            for k, at in enumerate(UP_CHUNKS):
                dve.wait_ge(up_hi, k + 1)
                dve.tensor_tensor(up_flat[1][:, at], stage[:, at], up_flat[0][:, at], ALU.subtract).then_inc(up_split, 1)
            dve.wait_ge(consts, 4)
            dve.wait_ge(small_loaded, len(small) * DMA_INC + DMA_INC)

            def lo(b, n, dst, src):
                dve.wait_ge(hid_hi, b * HID + NS + n + 1)
                dve.tensor_tensor(dst[1][:], src, dst[0][:], ALU.subtract).then_inc(hid_split, 1)

            def ranks(b):
                dve.wait_ge(logit_t_psum, b + 1)
                dve.tensor_scalar(logit_t[:], psum[0:NG, LOGIT_T_BANK, :], bg[:], None, ALU.add).then_inc(logit_t_ready, 1)
                dve.wait_ge(logit_psum, b + 1)
                dve.tensor_copy(logit[:].rearrange("p t n -> p (t n)"), psum[:, LOGIT_BANK, 0:NT * NG]).then_inc(route, 1)
                dve.wait_ge(route, b * ROUTE + 1)
                by_j = logit[:].rearrange("p t (i n) -> p t i n", i=1).to_broadcast([P, NT, NG, NG])
                by_i = logit[:].rearrange("p t (n i) -> p t n i", i=1).to_broadcast([P, NT, NG, NG])
                dve.tensor_tensor(above[:], by_j, by_i, ALU.is_gt).then_inc(route, 1)
                dve.tensor_tensor(equal[:], by_j, by_i, ALU.is_equal).then_inc(route, 1)
                dve.tensor_reduce(top[:], logit[:], AX_X, ALU.max).then_inc(route, 1)
                dve.wait_ge(route, b * ROUTE + 4)
                dve.tensor_tensor(shifted[:], logit[:], top[:].rearrange("p (t i) -> p t i", i=1).to_broadcast([P, NT, NG]),
                                  ALU.subtract).then_inc(shifted_ready, 1)
                for t in range(NT):
                    last = dve.tensor_tensor(equal[:, t, :, :], equal[:, t, :, :], earlier[:], ALU.mult)
                last.then_inc(route, 1)
                dve.wait_ge(route, b * ROUTE + 5)
                dve.tensor_tensor(above[:], above[:], equal[:], ALU.add).then_inc(route, 1)
                dve.wait_ge(route, b * ROUTE + 6)
                dve.tensor_reduce(rank[:], above[:], AX_X, ALU.add).then_inc(route, 1)

            def weights(b):
                dve.wait_ge(route, b * ROUTE + 7)
                dve.wait_ge(weight_exp, b + 1)
                dve.scalar_tensor_tensor(out=kept[:], in0=rank[:], scalar=float(KEPT), in1=weight[:],
                                         op0=ALU.is_lt, op1=ALU.mult).then_inc(route, 1)
                dve.wait_ge(route, b * ROUTE + 8)
                dve.tensor_reduce(total[:], kept[:], AX_X, ALU.add).then_inc(route, 1)
                dve.wait_ge(route, b * ROUTE + 9)
                dve.reciprocal(inv_total[:], total[:]).then_inc(weight_ready, 1)
                dve.wait_ge(weight_ready, b * 2 + 1)
                dve.tensor_tensor(weight1[:, :, 0:NE], kept[:, :, 0:NE],
                                  inv_total[:].rearrange("p (t i) -> p t i", i=1).to_broadcast([P, NT, NE]),
                                  ALU.mult).then_inc(weight_ready, 1)

            def glu(b, n):
                dve.wait_ge(up_psum, b * UP + NS + 2 * n + 2)
                dve.wait_ge(silu_done, b * HID + NS + n + 1)
                dve.scalar_tensor_tensor(out=hid32[:, n % 2, :], in0=psum[:, 2 + n % 2, :], scalar=b_up[:, n:n + 1],
                                         in1=gated[:, n % 2, :], op0=ALU.add, op1=ALU.mult).then_inc(glu_done, 1)

            def add_expert(b, n):
                if n == 0:
                    dve.wait_ge(f_read, b + 1)
                    dve.wait_ge(weight_ready, b * 2 + 2)
                dve.wait_ge(down_psum, b * DOWN + (n + 1 if n < NE - 1 else DOWN))
                src = y_bank(n % 2 if n < NE - 2 else 1)
                for t in range(NT):
                    w = weight1[:, t, n:n + 1]
                    if n == 0:
                        last = dve.tensor_scalar(f[:, t, :], src[:, t, :], w, None, ALU.mult)
                    else:
                        last = dve.scalar_tensor_tensor(out=f[:, t, :], in0=src[:, t, :], scalar=w, in1=f[:, t, :],
                                                        op0=ALU.mult, op1=ALU.add)
                last.then_inc(summed, 1)

            def add_shared(b):
                dve.wait_ge(down_psum, b * DOWN + DOWN - 1)
                for k in range(2):
                    last = dve.tensor_tensor(f[:, 2 * k:2 * k + 2, :], y_bank(0)[:, 2 * k:2 * k + 2, :],
                                             f[:, 2 * k:2 * k + 2, :], ALU.add)
                last.then_inc(summed, 1)

            def batch(b, last=False):
                ranks(b)
                for n in range(NE):
                    glu(b, n)
                    if n == 0:
                        weights(b)
                    if 1 <= n <= len(LAYER_NORM_PARTS) and not last:
                        LAYER_NORM_PARTS[n - 1](b)
                    lo(b, n, hid[n % 2], hid32[:, n % 2, :])
                    if n >= 1:
                        dve.wait_ge(summed, b * DOWN + n)
                        add_expert(b, n - 1)
                dve.wait_ge(summed, b * DOWN + NE)
                add_shared(b)
                dve.wait_ge(summed, b * DOWN + NE + 1)
                add_expert(b, NE - 1)

            with dve.Fori(0, B - 1) as b:
                batch(b)
            batch(B - 1, last=True)
            dve.wait_ge(summed, B * DOWN + 1)
            dve.wait_ge(y_free, B * DMA_INC)
            dve.wait_ge(xres_loaded, B * DMA_INC)
            for k in range(2):
                at = slice(k * NT // 2, (k + 1) * NT // 2)
                gate = gates[:, B - 1:B, D:2 * D].to_broadcast([P, NT // 2, D])
                dve.tensor_tensor(y[:, at, :], f[:, at, :], gate, ALU.mult).then_inc(last_gated, 1)
                dve.wait_ge(last_gated, k + 1)
                dve.tensor_tensor(y[:, at, :], y[:, at, :], xres[:, at, :], ALU.add).then_inc(y_ready, 1)

        @block.tensor
        def _(pe):
            def split_product(out, stationary, moving, start, stop):
                for n, (s, m) in enumerate(PASSES):
                    last = pe.matmul(out, stationary(s), moving(m), start=start and n == 0,
                                     stop=stop and n == len(PASSES) - 1)
                return last

            def layer_norm_transposes(b):
                pe.wait_ge(ln_ready, b + 1)
                for c in range(DC):
                    for t in range(NT):
                        last = pe.transpose(psum[:, Y_BANK[0] + c, t * P:(t + 1) * P],
                                            xin[:, t, c * P:(c + 1) * P], ident[:])
                    last.then_inc(ln_psum, 1)

            def up_product(k, bank):
                if k == 0 or k in UP_ENDS:
                    pe.wait_ge(up_split, 1 + (k and 1 + UP_ENDS.index(k)))
                for c in range(DC):
                    last = split_product(psum[:, bank, :], lambda s: up[s][:, k, c, :], lambda m: ht[m][:, c, :],
                                         c == 0, c == DC - 1)
                last.then_inc(up_psum, 1)

            def down_product(b, n):
                pe.wait_ge(hid_split, b * NE + n + 1)
                if n == 0:
                    pe.wait_ge(down_split, 2)
                dst = y_bank(n % 2 if n < NE - 2 else 1)
                for t in range(NT):
                    last = split_product(dst[:, t, :], lambda s: hid[n % 2][s][:, t * P:(t + 1) * P],
                                         lambda m: down[m][:, n, :], True, True)
                last.then_inc(down_psum, 1)

            def shared_down_product(b):
                pe.wait_ge(shid_split, b * NS + NS)
                pe.wait_ge(weight_t_ready, b + 1)
                for t in range(NT):
                    dst = y_bank(0)[:, t, :]
                    for m in range(NS):
                        split_product(dst, lambda s: shid[m][s][:, t * P:(t + 1) * P],
                                      lambda k: down[k][:, NE + m, :], m == 0, False)
                    last = pe.matmul(dst, weight_t[:, t * P:(t + 1) * P], b_out[:], start=False, stop=True)
                last.then_inc(down_psum, 1)

            def batch(b, last=False):
                for c in range(DC):
                    mm = pe.matmul(psum[0:NG, LOGIT_T_BANK, :], wg[:, c, :], ht32[:, c, :],
                                   start=(c == 0), stop=(c == DC - 1))
                mm.then_inc(logit_t_psum, 1)
                pe.wait_ge(ht_split, b + 1)
                up_product(0, 0)
                alone(pe, logit_t_ready, b + 1)
                for t in range(NT):
                    mm = pe.transpose(psum[:, LOGIT_BANK, t * NG:(t + 1) * NG], logit_t[:, t * P:(t + 1) * P],
                                      ident[0:NG, 0:NG])
                mm.then_inc(logit_psum, 1)
                up_product(1, 1)
                for n in range(NE):
                    if n < 2:
                        pe.wait_ge(silu_done, b * HID + n + 1)
                    up_product(NS + 2 * n, n % 2)
                    if n == 1:
                        pe.wait_ge(route, b * ROUTE + 1)
                    up_product(NS + 2 * n + 1, 2 + n % 2)
                    if n == 1:
                        pe.wait_ge(summed, b * DOWN + 1)
                        pe.wait_ge(weight_ready, b * 2 + 2)
                        for t in range(NT):
                            mm = pe.transpose(psum[0:NE + 1, WEIGHT_T_BANK, t * P:(t + 1) * P], weight1[:, t, :], ident[:])
                        mm.then_inc(weight_t_psum, 1)
                    if n >= 1:
                        if n == 2:
                            pe.wait_ge(weight_t_ready, b + 1)
                        if n >= 3:
                            pe.wait_ge(summed, b * DOWN + (n if n == NE - 1 else n - 1))
                        down_product(b, n - 1)
                    if n == NE - 2 and not last:
                        pe.wait_ge(summed, b * DOWN + 4)
                        layer_norm_transposes(b)
                if last:
                    pe.wait_ge(summed, b * DOWN + 4)
                else:
                    pe.wait_ge(ht32_ready, b * DC + DC)
                shared_down_product(b)
                pe.wait_ge(summed, b * DOWN + NE)
                down_product(b, NE - 1)

            pe.wait_ge(small_loaded, len(small) * DMA_INC + DMA_INC)
            pe.wait_ge(consts, 4)
            with pe.Fori(0, B - 1) as b:
                batch(b)
            batch(B - 1, last=True)


def adaln_block(nc, x, wqk_d, wv_d, wo_d, c_d, wmod_d, up_d, down_d, wg_d, bg_d, bgate_d, bup_d, bsup_d, bdown_d,
                bsdown_d, out):
    B, SEQ, D = x.shape
    x1 = nc.dram_tensor("x1_dram", [B, SEQ, D], F32).ap()
    NT = SEQ // P
    DC = D // P
    NE, NS = bgate_d.shape[1], bsup_d.shape[1]
    with ExitStack() as ctx:
        def sb(name, shape, dt=F32):
            return ctx.enter_context(nc.sbuf_tensor(name, shape, dt))

        psum = ctx.enter_context(nc.psum_tensor("psum", [P, 8, 512], F32))
        stage = sb("stage", [P, wo_d.shape[1]])
        mod_t = sb("mod_t", [P, 4 * DC, B])
        gates = sb("gates", [P, B, 2 * D])
        ident = sb("ident", [P, P])
        xin = sb("xin", [P, NT, D])
        ht32 = sb("ht32", [P, DC, SEQ])
        ht = [sb("ht_hi", [P, DC, SEQ], F32R), sb("ht_lo", [P, DC, SEQ], F32R)]
        xres = sb("xres", [P, NT, D])
        y = sb("y", [P, NT, D])
        wg = sb("wg", wg_d.shape)
        bg = sb("bg", bg_d.shape)
        b_gate = sb("b_gate", bgate_d.shape)
        b_up = sb("b_up", bup_d.shape)
        b_sup = sb("b_sup", bsup_d.shape)
        b_out = sb("b_out", [NE + 1, D])
        up_loaded, small_loaded, y_free = [ctx.enter_context(nc.semaphore(name))
                                           for name in ("up_loaded", "small_loaded", "y_free")]
        shared = (psum, stage, mod_t, gates, ident, xin, ht32, ht, xres, y, up_loaded, small_loaded, y_free)
        loads = ((wg[:], wg_d), (bg[:], bg_d), (b_gate[:], bgate_d), (b_up[:], bup_d), (b_sup[:], bsup_d),
                 (b_out[0:NE, :], bdown_d), (b_out[NE:NE + 1, :], bsdown_d))
        attention_layer(nc, shared, x, wqk_d, wv_d, wo_d, c_d, wmod_d, up_d, loads, x1)
        feed_forward_layer(nc, shared, (wg, bg, b_gate, b_up, b_sup, b_out), x1, down_d, out)


def kernel(**inputs):
    import numpy as np
    import concourse.bacc as bacc
    from concourse.bass_utils import run_bass_kernel_spmd

    def get(name):
        return np.asarray(inputs["L0_" + name])

    x = get("attn_x")
    B, SEQ, D = x.shape
    H, E, _ = get("attn_W_Q").shape
    DC = D // P
    NE, _, HID = get("ffn_Wgate").shape
    NS = get("ffn_Ws_up").shape[1] // P

    def qk_layout(w):
        return w.reshape(H, E, DC, P).transpose(3, 0, 2, 1)

    def up_layout(w, n):
        return w.reshape(n, DC, P, HID).transpose(2, 0, 1, 3)

    experts = np.stack([up_layout(get("ffn_Wgate"), NE), up_layout(get("ffn_Wup"), NE)], 2)
    shared = get("ffn_Ws_up").reshape(DC, P, NS, HID).transpose(1, 2, 0, 3)
    arrays = {
        "x": x,
        "wqk": np.stack([qk_layout(get("attn_W_Q")), qk_layout(get("attn_W_K"))], 2).reshape(P, H, 2 * DC * E),
        "wv": get("attn_W_V").reshape(H // 2, 2, E, DC, P).transpose(4, 0, 3, 1, 2).reshape(P, H * DC * E),
        "wo": get("attn_W_O").transpose(2, 0, 1).reshape(P, H * D),
        "c": get("c").reshape(B, DC, P).transpose(2, 1, 0),
        "wmod": get("wmod").reshape(DC, P, 6 * D).transpose(1, 0, 2).reshape(P, DC * 6 * D),
        "up": np.concatenate([shared.reshape(P, -1), experts.reshape(P, -1)], 1),
        "down": np.concatenate([get("ffn_Wdown").transpose(1, 0, 2).reshape(P, -1),
                                get("ffn_Ws_down").reshape(NS, P, D).transpose(1, 0, 2).reshape(P, -1)], 1),
        "wg": get("ffn_Wg").reshape(DC, P, -1).transpose(1, 0, 2),
        "bg": get("ffn_bg").reshape(-1, 1),
        "bgate": get("ffn_bgate").transpose(1, 0),
        "bup": get("ffn_bup").transpose(1, 0),
        "bsup": get("ffn_bs_up").reshape(NS, P).transpose(1, 0),
        "bdown": get("ffn_bdown"),
        "bsdown": get("ffn_bs_down").reshape(1, D),
    }
    nc = bacc.Bacc("TRN2", target_bir_lowering=False, num_devices=1)
    launch, args = {}, []
    for name, a in arrays.items():
        a = np.ascontiguousarray(a)
        launch[f"in_{name}"] = a
        args.append(nc.dram_tensor(f"in_{name}", a.shape, mybir.dt.from_np(a.dtype), kind="ExternalInput").ap())
    args.append(nc.dram_tensor("block_out", x.shape, F32, kind="ExternalOutput").ap())
    adaln_block(nc, *args)
    r = run_bass_kernel_spmd(nc, [launch], core_ids=[0])
    return r.results[0]["block_out"]
```
